# Optimizing a Trainium2 kernel written in Bass

```python
import numpy as np
import jax
import jax.numpy as jnp

def _softmax(x, axis=-1):
    return jax.nn.softmax(x, axis=axis)

def _gelu(x):
    return jax.nn.gelu(x, approximate=True)

def _silu(x):
    return jax.nn.silu(x)

def _sigmoid(x):
    return jax.nn.sigmoid(x)

def _layernorm(x, axis=-1, eps=1e-05):
    m = jnp.mean(x, axis=axis, keepdims=True)
    v = jnp.var(x, axis=axis, keepdims=True)
    return (x - m) / jnp.sqrt(v + eps)

def _scatter_add(tgt, idx, src, axis=0):
    return tgt.at[idx].add(src)

def _segment_sum(src, seg, n):
    return jax.ops.segment_sum(src, seg, n)
kernel_name = 'mk_macaron_d1_jaxref_r8_6ebb4d'

def setup_inputs(seed: int=0):
    np.random.seed(seed)
    _w = jnp.asarray

    def _L0_attn_setup():
        import jax, jax.numpy as jnp
        import numpy as np
        D_MODEL = 256
        N_HEADS = 16
        SEQ_LEN = 256
        BATCH = 2
        BIAS_MAX = 8.0

        def alibi_bias(n_heads, seq_len, dtype):
            pos = jnp.arange(1 - seq_len, 1, dtype=dtype)
            m = jnp.arange(1, n_heads + 1, dtype=dtype) * (BIAS_MAX / n_heads)
            slopes = 1.0 / 2.0 ** m
            return pos[None, :] * slopes[:, None]
        key = jax.random.key(seed)
        k1, k2, k3 = jax.random.split(key, 3)
        s = 1.0 / np.sqrt(D_MODEL)
        x = jax.random.normal(k1, (BATCH, SEQ_LEN, D_MODEL), dtype=jnp.float32)
        Wqkv = jax.random.normal(k2, (3 * D_MODEL, D_MODEL), dtype=jnp.float32) * s
        b_qkv = jnp.zeros((3 * D_MODEL,), dtype=jnp.float32)
        Wout = jax.random.normal(k3, (D_MODEL, D_MODEL), dtype=jnp.float32) * s
        b_out = jnp.zeros((D_MODEL,), dtype=jnp.float32)
        return {'x': x, 'Wqkv': Wqkv, 'b_qkv': b_qkv, 'Wout': Wout, 'b_out': b_out}
    _L0_attn_in = _L0_attn_setup()

    def _L0_ffn_setup():
        import jax, jax.numpy as jnp
        import numpy as np
        BLOCK_SIZE = 32
        HIDDEN_SIZE = 256
        MLP_DIM = 2048
        NVFP4_LUT = jnp.array([0.0, 0.5, 1.0, 1.5, 2.0, 3.0, 4.0, 6.0, 0.0, -0.5, -1.0, -1.5, -2.0, -3.0, -4.0, -6.0], dtype=jnp.float32)

        def dequant_nvfp4(W_packed, scales, block=BLOCK_SIZE):
            N = W_packed.shape[0]
            low = W_packed & 15
            high = W_packed >> 4 & 15
            idx = jnp.stack([low, high], axis=-1).reshape(N, -1)
            vals = NVFP4_LUT[idx]
            K = vals.shape[1]
            vals = vals.reshape(N, K // block, block) * scales[:, :, None]
            return vals.reshape(N, K)
        key = jax.random.key(seed)
        ks = jax.random.split(key, 7)
        x = jax.random.normal(ks[0], (4, 32, HIDDEN_SIZE), dtype=jnp.float32)
        gate_W_packed = jax.random.randint(ks[1], (MLP_DIM, HIDDEN_SIZE // 2), 0, 32, dtype=jnp.int32)
        gate_scales = jax.random.uniform(ks[2], (MLP_DIM, HIDDEN_SIZE // BLOCK_SIZE), dtype=jnp.float32) * 0.1 + 0.001
        up_W_packed = jax.random.randint(ks[3], (MLP_DIM, HIDDEN_SIZE // 2), 0, 32, dtype=jnp.int32)
        up_scales = jax.random.uniform(ks[4], (MLP_DIM, HIDDEN_SIZE // BLOCK_SIZE), dtype=jnp.float32) * 0.1 + 0.001
        down_W_packed = jax.random.randint(ks[5], (HIDDEN_SIZE, MLP_DIM // 2), 0, 32, dtype=jnp.int32)
        down_scales = jax.random.uniform(ks[6], (HIDDEN_SIZE, MLP_DIM // BLOCK_SIZE), dtype=jnp.float32) * 0.1 + 0.001
        return {'x': x, 'gate_W_packed': gate_W_packed, 'gate_scales': gate_scales, 'up_W_packed': up_W_packed, 'up_scales': up_scales, 'down_W_packed': down_W_packed, 'down_scales': down_scales}
    _L0_ffn_in = _L0_ffn_setup()
    _d = {'L0_attn_x': _L0_attn_in['x'], 'L0_attn_Wqkv': _L0_attn_in['Wqkv'], 'L0_attn_b_qkv': _L0_attn_in['b_qkv'], 'L0_attn_Wout': _L0_attn_in['Wout'], 'L0_attn_b_out': _L0_attn_in['b_out'], 'L0_ffn_gate_W_packed': _L0_ffn_in['gate_W_packed'], 'L0_ffn_gate_scales': _L0_ffn_in['gate_scales'], 'L0_ffn_up_W_packed': _L0_ffn_in['up_W_packed'], 'L0_ffn_up_scales': _L0_ffn_in['up_scales'], 'L0_ffn_down_W_packed': _L0_ffn_in['down_W_packed'], 'L0_ffn_down_scales': _L0_ffn_in['down_scales']}
    _x0 = _d['L0_attn_x']
    _d['L0_attn_x'] = jax.random.normal(jax.random.fold_in(jax.random.key(seed), 1), (8, 256, 256), dtype=_x0.dtype)
    del _x0
    return _d

def reference(L0_attn_x, L0_attn_Wqkv, L0_attn_b_qkv, L0_attn_Wout, L0_attn_b_out, L0_ffn_gate_W_packed, L0_ffn_gate_scales, L0_ffn_up_W_packed, L0_ffn_up_scales, L0_ffn_down_W_packed, L0_ffn_down_scales):

    def _L0_attn_ref(x, Wqkv, b_qkv, Wout, b_out):
        import jax, jax.numpy as jnp
        import numpy as np
        D_MODEL = 256
        N_HEADS = 16
        SEQ_LEN = 256
        BATCH = 2
        BIAS_MAX = 8.0

        def alibi_bias(n_heads, seq_len, dtype):
            pos = jnp.arange(1 - seq_len, 1, dtype=dtype)
            m = jnp.arange(1, n_heads + 1, dtype=dtype) * (BIAS_MAX / n_heads)
            slopes = 1.0 / 2.0 ** m
            return pos[None, :] * slopes[:, None]
        B, S, D = x.shape
        H = N_HEADS
        hd = D // H
        scale = 1.0 / jnp.sqrt(jnp.asarray(hd, dtype=x.dtype))
        qkv = x @ Wqkv.T + b_qkv
        q, k, v = jnp.split(qkv, 3, axis=-1)
        q = q.reshape(B, S, H, hd)
        k = k.reshape(B, S, H, hd)
        v = v.reshape(B, S, H, hd)
        scores = jnp.einsum('bqhd,bkhd->bhqk', q, k) * scale
        bias = alibi_bias(H, S, x.dtype)
        scores = scores + bias[None, :, None, :]
        causal = jnp.tril(jnp.ones((S, S), dtype=bool))
        scores = jnp.where(causal[None, None, :, :], scores, jnp.asarray(-1000000000.0, dtype=x.dtype))
        p = jax.nn.softmax(scores, axis=-1)
        ctx = jnp.einsum('bhqk,bkhd->bqhd', p, v).reshape(B, S, D)
        return ctx @ Wout.T + b_out

    def _L0_ffn_ref(x, gate_W_packed, gate_scales, up_W_packed, up_scales, down_W_packed, down_scales):
        import jax, jax.numpy as jnp
        import numpy as np
        BLOCK_SIZE = 32
        HIDDEN_SIZE = 256
        MLP_DIM = 2048
        NVFP4_LUT = jnp.array([0.0, 0.5, 1.0, 1.5, 2.0, 3.0, 4.0, 6.0, 0.0, -0.5, -1.0, -1.5, -2.0, -3.0, -4.0, -6.0], dtype=jnp.float32)

        def dequant_nvfp4(W_packed, scales, block=BLOCK_SIZE):
            N = W_packed.shape[0]
            low = W_packed & 15
            high = W_packed >> 4 & 15
            idx = jnp.stack([low, high], axis=-1).reshape(N, -1)
            vals = NVFP4_LUT[idx]
            K = vals.shape[1]
            vals = vals.reshape(N, K // block, block) * scales[:, :, None]
            return vals.reshape(N, K)
        B, S, H = x.shape
        xt = x.reshape(B * S, H)
        Wg = dequant_nvfp4(gate_W_packed, gate_scales)
        Wu = dequant_nvfp4(up_W_packed, up_scales)
        Wd = dequant_nvfp4(down_W_packed, down_scales)
        gate = jnp.einsum('th,nh->tn', xt, Wg)
        up = jnp.einsum('th,nh->tn', xt, Wu)
        gelu = jnp.tanh(0.7978845608028654 * (gate + 0.044715 * gate ** 3)) * gate * 0.5 + gate * 0.5
        inter = gelu * up
        out = jnp.einsum('tn,hn->th', inter, Wd)
        return out.reshape(B, S, H)
    x = L0_attn_x
    x = x + 0.5 * _L0_ffn_ref(_layernorm(x, axis=-1), L0_ffn_gate_W_packed, L0_ffn_gate_scales, L0_ffn_up_W_packed, L0_ffn_up_scales, L0_ffn_down_W_packed, L0_ffn_down_scales)
    x = x + _L0_attn_ref(_layernorm(x, axis=-1), L0_attn_Wqkv, L0_attn_b_qkv, L0_attn_Wout, L0_attn_b_out)
    x = x + 0.5 * _L0_ffn_ref(_layernorm(x, axis=-1), L0_ffn_gate_W_packed, L0_ffn_gate_scales, L0_ffn_up_W_packed, L0_ffn_up_scales, L0_ffn_down_W_packed, L0_ffn_down_scales)
    return x

_drawn_inputs = setup_inputs


def setup_inputs(seed=0):
    import zlib

    import numpy as np

    out = dict(_drawn_inputs(seed))
    spreads = {'L0_attn_b_qkv': (0.0, 0.49), 'L0_attn_b_out': (0.0, 0.492)}
    factors = {}
    for name, (base, spread) in spreads.items():
        noise = np.random.default_rng([zlib.crc32(name.encode()), seed]).standard_normal(out[name].shape)
        drawn = base * np.exp(spread * noise) if base else spread * noise
        out[name] = jnp.asarray(drawn.astype(out[name].dtype))
    for name, factor in factors.items():
        out[name] = (out[name] * factor).astype(out[name].dtype)
    return out
```

```python
from contextlib import ExitStack

import numpy as np

import concourse.bass as bass
from concourse import mybir

F32, F32R, F16, BF16, I32 = (mybir.dt.float32, mybir.dt.float32r, mybir.dt.float16,
                             mybir.dt.bfloat16, mybir.dt.int32)
ALU = mybir.AluOpType
ACT = mybir.ActivationFunctionType
AX = mybir.AxisListType

P = 128
D = 256
KT = D // P
MLP = 2048
NT = MLP // P
B, S = 8, 256
TILE = 512
TILES = B * S // TILE
SUB = TILE // P
H, HD = 16, 16
PAIRS = H // 2
HALF = PAIRS // 2
CH = 512
CHUNKS = MLP // CH
NCH = CH // P
EPS = 1e-5
EXP_SHIFT = 15 * float(np.log(2.0))
MASKED = -1e30
VP = 3 * HD + 1
VW = 64


def macaron_kernel(nc, x, gate_pk, gate_sc, up_pk, up_sc, down_pk, down_sc, wqkv, bqk, bv, wout, bout, aux, out):
    ctx = ExitStack()
    with ctx:
        cursor = [nc.sbuf_base]

        def place(name, shape, dt, at=None):
            size = int(np.prod(shape[1:])) * (2 if dt in (F16, BF16) else 4)
            if at is None:
                at = (cursor[0] + 31) // 32 * 32
                cursor[0] = at + size
            return nc.alloc_sbuf_tensor_at(name, shape, dt, offset=at), at + size

        def sb(name, shape, dt):
            return place(name, shape, dt)[0]

        def sem(name):
            return ctx.enter_context(nc.semaphore(name))

        WG = sb("WG", [P, 2, KT, MLP], F32R)
        WU = sb("WU", [P, 2, KT, MLP], F32R)
        WD = sb("WD", [P, NT, 2, D], F32R)
        WQ = sb("WQ", [P, 2, KT, 3 * D], F32R)
        WO = sb("WO", [P, 2, KT, D], F32R)
        X = sb("X", [P, TILES * SUB, D], F32)
        yT = sb("yT", [P, 2, KT, TILE], F32R)
        yn = sb("yn", [P, SUB, D], F32)
        ident = sb("ident", [P, P], F32)
        identb = sb("identb", [P, P], BF16)
        mask = sb("mask", [P, 2, P], BF16)
        maskT = sb("maskT", [P, 2, P], BF16)
        bqk_sb = sb("bqk_sb", [P, 4], F32)
        bqk_s = sb("bqk_s", [P, 4], F32)
        bv_sb = sb("bv_sb", [P, D], F32)
        bo_sb = sb("bo_sb", [P, D], F32)
        st6 = sb("st6", [P, SUB, 6], F32)
        mv = sb("mv", [P, SUB, 2], F32)
        ve = sb("ve", [P, SUB], F32)
        rstd = sb("rstd", [P, SUB], F32)
        mhalf = sb("mhalf", [P, SUB], F32)
        epst = sb("epst", [P, SUB], F32)
        carry = sb("carry", [P, 1], F32)
        shift = sb("shift", [P, 1], F32)
        mx = sb("mx", [P, 2, 2, 2, HALF], F32)
        NM = sb("NM", [P, 2, 2, 2, 2, HALF], F32)
        rc = sb("rc", [P, 2, 8], F32)
        region = (cursor[0] + 31) // 32 * 32
        QS, e = place("QS", [P, PAIRS, S], F32R, region)
        KS, region2 = place("KS", [P, PAIRS, S], F32R, e)
        pk, e = place("pk", [P, 2, CH], I32, region)
        sc, e = place("sc", [P, 2, CH], F32, e)
        dT, e = place("dT", [P, 2, CH], I32, e)
        dU, e = place("dU", [P, 2, CH], I32, e)
        assert e <= region2
        ih, e = place("ih", [P, 3, TILE], F32R, region2)
        il, e = place("il", [P, 3, TILE], F32R, e)
        gb, e = place("gb", [P, 2, TILE], F32, e)
        tb, e = place("tb", [P, 2, TILE], F32, e)
        wf, e = place("wf", [P, 2, CH], F32, e)
        wqs, e = place("wqs", [P, KT, 3 * D], F32, e)
        wos, e = place("wos", [P, KT, D], F32, e)
        end_a = e
        HL, e = place("HL", [P, 4, 2, S], F32R, region2)
        v32, e = place("v32", [P, 2, D], F32, e)
        vr, e = place("vr", [P, 2, D], F32, e)
        Vx, e = place("Vx", [P, 2, H, VW], BF16, e)
        Pf, e = place("Pf", [P, 2, 2, 384], F32, e)
        Ph, e = place("Ph", [P, 2, 2, 384], F16, e)
        Pl, e = place("Pl", [P, 2, 2, 384], F16, e)
        cs, e = place("cs", [P, 2, 8, HD], F32, e)
        cx, e = place("cx", [P, 2, D], F32, e)
        CT, e = place("CT", [P, 2, KT, S], F32R, e)
        MT, e = place("MT", [16, 2, S], F32R, e)
        auxs, _ = place("auxs", [16, PAIRS, S], F32, region2)
        auxr, _ = place("auxr", [16, PAIRS, S], F32R, region2 + PAIRS * S * 4)
        assert max(e, end_a) <= nc.sbuf_usable_end, (e, end_a, nc.sbuf_usable_end)

        ps = ctx.enter_context(nc.psum_tensor("ps", [P, 8, 512], F32))

        x_first = sem("x_first")
        x_rest = sem("x_rest")
        pk_in = [sem(f"pk_in{b}") for b in range(2)]
        sc_in = [sem(f"sc_in{b}") for b in range(2)]
        wa_in = sem("wa_in")
        aux_in = sem("aux_in")
        const_done = sem("const_done")
        const_init = sem("const_init")
        vx_ones = sem("vx_ones")
        dec1 = sem("dec1")
        dec2 = sem("dec2")
        w_f = sem("w_f")
        w_hi = sem("w_hi")
        w_lo = sem("w_lo")
        wa_hi = sem("wa_hi")
        wa_lo = sem("wa_lo")
        bn1 = sem("bn1")
        bn2 = sem("bn2")
        ve_done = sem("ve_done")
        rstd_done = sem("rstd_done")
        yn_done = sem("yn_done")
        xt_done = sem("xt_done")
        yh_done = sem("yh_done")
        yl_done = sem("yl_done")
        g_ready = sem("g_ready")
        u_ready = sem("u_ready")
        gelu_done = sem("gelu_done")
        inter_done = sem("inter_done")
        hi_done = sem("hi_done")
        lo_done = sem("lo_done")
        d_done = sem("d_done")
        xa_done = sem("xa_done")
        x_done = sem("x_done")
        aux_r = sem("aux_r")
        aux_st = sem("aux_st")
        qk_ready = sem("qk_ready")
        qk_hi = sem("qk_hi")
        qk_lo = sem("qk_lo")
        v_ready = sem("v_ready")
        v_sum = sem("v_sum")
        v_1 = sem("v_1")
        v_r = sem("v_r")
        v_2 = sem("v_2")
        v_3 = sem("v_3")
        stk = sem("stk")
        s_ready = sem("s_ready")
        mx_done = sem("mx_done")
        nm_done = sem("nm_done")
        mt_ready = sem("mt_ready")
        mt_copied = sem("mt_copied")
        m_rows = [sem(f"m_rows{h}") for h in range(2)]
        st_ready = sem("st_ready")
        exp_done = sem("exp_done")
        pl_done = sem("pl_done")
        pv_done = sem("pv_done")
        red_done = sem("red_done")
        rc_done = sem("rc_done")
        cx_done = sem("cx_done")
        ct_ready = sem("ct_ready")
        ct_hi = sem("ct_hi")
        ct_lo = sem("ct_lo")
        o_ready = sem("o_ready")
        xb_done = sem("xb_done")
        ax_done = sem("ax_done")
        stored = sem("stored")

        ROUNDS = [(w, c) for c in range(CHUNKS) for w in range(3)]

        def codes(w, c):
            return (gate_pk, up_pk, down_pk)[w][:, c * CH:(c + 1) * CH]

        def scales(w, c):
            return (gate_sc, up_sc, down_sc)[w][:, c * CH:(c + 1) * CH]

        def weights(w, c, par, part):
            if w < 2:
                return (WG, WU)[w][:, part, par, c * CH:(c + 1) * CH]
            return WD[:, 2 * (2 * c) + par:2 * (2 * c + 1) + par + 1:2, part, :]

        def split2(ap, w):
            return ap if w < 2 else ap.rearrange("p (j h) -> p j h", j=2)

        block = ctx.enter_context(nc.Block())

        @block.sync
        def _(sp):
            xv = x.rearrange("b (s p) d -> p (b s) d", p=P)
            ov = out.rearrange("b (s p) d -> p (b s) d", p=P)
            for r, (w, c) in enumerate(ROUNDS):
                if r >= 2:
                    sp.wait_ge(dec1, 2 * (r - 1))
                sp.dma_start(pk[:, r % 2, :], codes(w, c)).then_inc(pk_in[r % 2], 16)
                if r >= 2:
                    sp.wait_ge(w_f, 2 * (r - 1))
                sp.dma_start(sc[:, r % 2, :], scales(w, c)).then_inc(sc_in[r % 2], 16)
                if r == 0:
                    sp.dma_start(X[:, 0:SUB, :], xv[:, 0:SUB, :]).then_inc(x_first, 16)
                if r == 1:
                    sp.dma_start(X[:, SUB:, :], xv[:, SUB:, :]).then_inc(x_rest, 16)
            sp.dma_start(wqs[:], wqkv).then_inc(wa_in, 16)
            sp.dma_start(wos[:], wout).then_inc(wa_in, 16)
            sp.dma_start(bqk_sb[:], bqk).then_inc(wa_in, 16)
            sp.dma_start(bv_sb[:], bv.partition_broadcast(P)).then_inc(wa_in, 16)
            sp.dma_start(bo_sb[:], bout.partition_broadcast(P)).then_inc(wa_in, 16)
            sp.wait_ge(x_done, TILES)
            sp.dma_start(auxs[:], aux).then_inc(aux_in, 16)
            sp.wait_ge(aux_r, 1)
            for a in range(2):
                sp.dma_start(KS[64 * a + 48:64 * a + 52, :, :].bitcast(F32), auxr[4 * a:4 * a + 4, :, :].bitcast(F32)).then_inc(aux_st, 16)
                sp.dma_start(QS[64 * a + 48:64 * a + 50, :, :].bitcast(F32), auxr[8 + 2 * a:10 + 2 * a, :, :].bitcast(F32)).then_inc(aux_st, 16)

            def stack_rows(c):
                sp.wait_ge(st_ready, 8 * c)
                sp.wait_ge(qk_hi, 4 * c + 4)
                sp.wait_ge(qk_lo, 4 * c + 4)
                for t, dst in ((0, QS), (1, KS)):
                    for g, part in enumerate(((0, 0, 1), (0, 1, 0))[t]):
                        for a in range(2):
                            row = 64 * a + 16 * g
                            sp.dma_start(dst[row:row + HD, :, :].bitcast(F32),
                                         HL[:, 2 * t + a, part, :].bitcast(F32)).then_inc(stk, 16)

            def max_rows(c, hf):
                sp.wait_ge(mt_copied, 2 * c + hf + 1)
                for a in range(2):
                    for part in range(2):
                        r = 8 * a + 4 * part
                        sp.dma_start(QS[64 * a + 50 + part:64 * a + 51 + part, HALF * hf:HALF * hf + HALF, :].bitcast(F32),
                                     MT[r:r + 4, hf, :].bitcast(F32)).then_inc(m_rows[hf], 16)

            with sp.Fori(0, TILES) as i:
                for b in range(2):
                    stack_rows(2 * i + b)
                    max_rows(2 * i + b, 0)
                    max_rows(2 * i + b, 1)
            with sp.Fori(0, TILES) as i:
                first = sp.snap(SUB * i)
                sp.wait_ge(x_done, TILES + 1 + i)
                sp.dma_start(ov[:, bass.ds(first, SUB), :], X[:, bass.ds(first, SUB), :]).then_inc(stored, 16)
            sp.wait_ge(stored, 16 * TILES)

        @block.gpsimd
        def _(pool):
            for t, v in ((ident, 0.0), (identb, 0.0), (mask, 0.0), (maskT, 0.0), (mhalf, -0.5), (epst, EPS), (shift, EXP_SHIFT)):
                pool.memset(t[:], v).then_inc(const_init, 1)
            pool.wait_ge(const_init, 7)
            for t in (ident, identb):
                pool.affine_select(out=t[:, :], in_=t[:, :], compare_op=ALU.not_equal, fill=1.0, base=0,
                                   pattern=[[-1, P]], channel_multiplier=1).then_inc(const_done, 1)
            pool.affine_select(out=mask[:], in_=mask[:], compare_op=ALU.is_ge, fill=MASKED, base=0,
                               pattern=[[0, 2], [-1, P]], channel_multiplier=1).then_inc(const_done, 1)
            pool.affine_select(out=maskT[:], in_=maskT[:], compare_op=ALU.is_ge, fill=MASKED, base=0,
                               pattern=[[0, 2], [1, P]], channel_multiplier=-1).then_inc(const_done, 1)

            def inv_std(k):
                pool.wait_ge(bn2, SUB * (k + 1))
                pool.tensor_tensor(ve[:, :], mv[:, :, 1], epst[:, :], ALU.add).then_inc(ve_done, 1)
                pool.wait_ge(ve_done, k + 1)
                pool.tensor_tensor(rstd[:, :], ve[:, :], mhalf[:, :], ALU.pow).then_inc(rstd_done, 1)

            def w_low(r):
                w, c = ROUNDS[r]
                for par in range(2):
                    k = 2 * r + par
                    pool.wait_ge(w_hi, k + 1)
                    pool.tensor_tensor(weights(w, c, par, 1), split2(wf[:, par, :], w),
                                       weights(w, c, par, 0).bitcast(F32), ALU.subtract).then_inc(w_lo, 1)

            inv_std(0)
            for r in range(len(ROUNDS)):
                w_low(r)
                if r == 5:
                    inv_std(1)
            with pool.Fori(0, TILES - 1) as i:
                inv_std(2 + i)
            pool.wait_ge(aux_st, 64)
            pool.memset(Vx[:, :, :, 3 * HD], 1.0).then_inc(vx_ones, 1)
            with pool.Fori(0, TILES) as i:
                inv_std(TILES + 1 + i)
                for b in range(2):
                    c = 2 * i + b
                    pool.wait_ge(v_1, c + 1)
                    pool.tensor_tensor(vr[:], v32[:], Vx[:, :, :, 0:HD], ALU.subtract).then_inc(v_r, 1)
                    pool.wait_ge(v_2, c + 1)
                    pool.tensor_tensor(Vx[:, :, :, 2 * HD:3 * HD], vr[:], Vx[:, :, :, HD:2 * HD],
                                       ALU.subtract).then_inc(v_3, 1)
            with pool.Fori(0, TILES) as i:
                inv_std(2 * TILES + 1 + i)

        @block.scalar
        def _(act):
            def y_high(k, bank):
                act.wait_ge(xt_done, k + 1)
                for kt in range(KT):
                    act.activation(yT[:, 0, kt, :], ps[:, bank[kt], :], ACT.Copy).then_inc(yh_done, 1)

            def w_high(r):
                w, c = ROUNDS[r]
                for par in range(2):
                    k = 2 * r + par
                    act.wait_ge(w_f, k + 1)
                    act.activation(weights(w, c, par, 0), split2(wf[:, par, :], w), ACT.Copy).then_inc(w_hi, 1)

            def ffn_tile(t, k, first=False):
                for n in range(NT):
                    act.wait_ge(g_ready, NT * t + n + 1)
                    if n >= 2 or not first:
                        act.wait_ge(inter_done, NT * t + n - 1)
                    act.activation(gb[:, n % 2, :], ps[:, 4 + n % 2, :], ACT.Gelu_apprx_tanh).then_inc(gelu_done, 1)
                    act.wait_ge(inter_done, NT * t + n + 1)
                    if n == 0 and not first:
                        act.wait_ge(d_done, NT * t)
                    if n >= 3:
                        act.wait_ge(d_done, NT * t + n - 2)
                    act.activation(ih[:, n % 3, :], tb[:, n % 2, :], ACT.Copy).then_inc(hi_done, 1)
                    if first and n % NCH == 0 and n // NCH + 1 < CHUNKS:
                        for w in range(3):
                            w_high(3 * (n // NCH + 1) + w)
                y_high(k + 1, (4, 6))

            y_high(0, (4, 6))
            for w in range(3):
                w_high(w)
            ffn_tile(0, 0, first=True)
            act.wait_ge(wa_in, 80)
            act.activation(WQ[:, 0, :, 0:D], wqs[:, :, 0:D], ACT.Copy, scale=0.25).then_inc(wa_hi, 1)
            act.activation(WQ[:, 0, :, D:3 * D], wqs[:, :, D:3 * D], ACT.Copy).then_inc(wa_hi, 1)
            act.activation(WO[:, 0, :, :], wos[:], ACT.Copy).then_inc(wa_hi, 1)
            with act.Fori(0, TILES - 1) as i:
                ffn_tile(1 + i, 1 + i)
            act.wait_ge(aux_in, 16)
            act.activation(auxr[:], auxs[:], ACT.Copy).then_inc(aux_r, 1)

            def qk_high(c):
                act.wait_ge(stk, 192 * c)
                for b in range(4):
                    act.wait_ge(qk_ready, 4 * c + 2 * (b // 2) + 2)
                    act.activation(HL[:, b, 0, :], ps[:, 6 + b // 2, S * (b % 2):S * (b % 2) + S], ACT.Identity,
                                   bias=bqk_s[:, b:b + 1]).then_inc(qk_hi, 1)

            def v_parts(c):
                act.wait_ge(pv_done, 8 * c)
                act.wait_ge(v_sum, c + 1)
                act.activation(Vx[:, :, :, 0:HD], v32[:].rearrange("p t (h d) -> p t h d", h=H),
                               ACT.Copy).then_inc(v_1, 1)
                act.wait_ge(v_r, c + 1)
                act.activation(Vx[:, :, :, HD:2 * HD], vr[:].rearrange("p t (h d) -> p t h d", h=H),
                               ACT.Copy).then_inc(v_2, 1)

            def max_copy(c, hf):
                act.wait_ge(mt_ready, 2 * c + hf + 1)
                act.wait_ge(m_rows[hf], 64 * c)
                act.activation(MT[:, hf, :], ps[0:16, 7, 0:S], ACT.Copy).then_inc(mt_copied, 1)

            def exps(c, p):
                act.wait_ge(st_ready, 8 * c + p + 1)
                u = p % 2
                if p >= 2:
                    act.wait_ge(pv_done, 8 * c + p - 1)
                act.activation(Ph[:, u], ps[:, 2:4, 0:384], ACT.Exp, bias=shift[:, 0:1]).then_inc(exp_done, 1)
                if p >= 2:
                    act.wait_ge(pl_done, 8 * c + p - 1)
                act.activation(Pf[:, u], ps[:, 2:4, 0:384], ACT.Exp, bias=shift[:, 0:1]).then_inc(exp_done, 1)

            with act.Fori(0, TILES) as i:
                for b in range(2):
                    c = 2 * i + b
                    qk_high(c)
                    v_parts(c)
                    if b == 1:
                        y_high(TILES + 1 + i, (6, 7))
                    max_copy(c, 0)
                    max_copy(c, 1)
                    for p in range(PAIRS):
                        exps(c, p)
                    act.wait_ge(ct_ready, c + 1)
                    act.activation(CT[:, 0], ps[:, 6, :].rearrange("p (k t) -> p k t", k=KT),
                                   ACT.Copy).then_inc(ct_hi, 1)
            with act.Fori(0, TILES) as i:
                ffn_tile(TILES + i, 2 * TILES + i)

        @block.vector
        def _(dve):
            def stats(k, tile):
                for s in range(SUB):
                    dve.bn_stats(st6[:, s, :], X[:, bass.ds(SUB * tile + s, 1), :].rearrange("p s d -> p (s d)")).then_inc(bn1, 1)
                dve.wait_ge(bn1, SUB * (k + 1))
                dve.memset(carry[:], 0.0)
                for s in range(SUB):
                    dve.bn_aggr(mv[:, s, :], st6[:, s, :]).then_inc(bn2, 1)

            def normalise(k, tile):
                dve.wait_ge(rstd_done, k + 1)
                if not (isinstance(k, int) and k == 0):
                    dve.wait_ge(xt_done, k)
                for s in range(SUB):
                    dve.tensor_scalar(yn[:, s, :], X[:, bass.ds(SUB * tile + s, 1), :].rearrange("p s d -> p (s d)"),
                                      mv[:, s, 0:1], rstd[:, s:s + 1], ALU.subtract, ALU.mult).then_inc(yn_done, 1)

            def y_low(k, bank):
                for kt in range(KT):
                    dve.wait_ge(yh_done, KT * k + kt + 1)
                    dve.tensor_tensor(yT[:, 1, kt, :], ps[:, bank[kt], :], yT[:, 0, kt, :].bitcast(F32),
                                      ALU.subtract).then_inc(yl_done, 1)

            def dequant(r):
                w, c = ROUNDS[r]
                u = r % 2
                dve.wait_ge(pk_in[u], 16 * (r // 2 + 1))
                for par in range(2):
                    dve.tensor_scalar(dT[:, par, :], pk[:, u, :], 28 - 4 * par, 19, ALU.logical_shift_left,
                                      ALU.arith_shift_right).then_inc(dec1, 1)
                for par in range(2):
                    dve.wait_ge(dec1, 2 * r + par + 1)
                    dve.tensor_scalar(dU[:, par, :], dT[:, par, :], 0x8E00, None, ALU.bitwise_and).then_inc(dec2, 1)
                dve.wait_ge(sc_in[u], 16 * (r // 2 + 1))
                for par in range(2):
                    dve.wait_ge(dec2, 2 * r + par + 1)
                    if r >= 1:
                        dve.wait_ge(w_lo, 2 * (r - 1) + par + 1)
                    dve.scalar_tensor_tensor(out=wf[:, par, :], in0=dU[:, par, :].bitcast(F16)[:, 0::2],
                                             scalar=float(2 ** 14), in1=sc[:, u, :], op0=ALU.mult,
                                             op1=ALU.mult).then_inc(w_f, 1)

            def ffn_tile(t, k, tile, nxt, first=False):
                for n in range(NT):
                    dve.wait_ge(u_ready, NT * t + n + 1)
                    dve.wait_ge(gelu_done, NT * t + n + 1)
                    if n >= 2 or not first:
                        dve.wait_ge(hi_done, NT * t + n - 1)
                        dve.wait_ge(lo_done, NT * t + n - 1)
                    dve.tensor_tensor(tb[:, n % 2, :], ps[:, 6 + n % 2, :], gb[:, n % 2, :],
                                      ALU.mult).then_inc(inter_done, 1)
                    dve.wait_ge(hi_done, NT * t + n + 1)
                    dve.tensor_tensor(il[:, n % 3, :], tb[:, n % 2, :], ih[:, n % 3, :].bitcast(F32),
                                      ALU.subtract).then_inc(lo_done, 1)
                    if n == 4:
                        stats(k + 1, nxt)
                    if n == 7:
                        normalise(k + 1, nxt)
                    if first and n % NCH == 0 and n // NCH + 1 < CHUNKS:
                        for w in range(3):
                            dequant(3 * (n // NCH + 1) + w)
                y_low(k + 1, (4, 6))
                dve.wait_ge(d_done, NT * (t + 1))
                xt = X[:, bass.ts(tile, SUB), :]
                dve.scalar_tensor_tensor(out=xt, in0=ps[:, 0:4, 0:D], scalar=0.5, in1=xt, op0=ALU.mult,
                                         op1=ALU.add).then_inc(xa_done, 1)
                dve.wait_ge(xa_done, t + 1)
                dve.scalar_tensor_tensor(out=xt, in0=ps[:, 0:4, D:2 * D], scalar=0.5, in1=xt, op0=ALU.mult,
                                         op1=ALU.add).then_inc(x_done, 1)

            dve.wait_ge(x_first, 16)
            stats(0, 0)
            dequant(0)
            normalise(0, 0)
            dequant(1)
            y_low(0, (4, 6))
            dequant(2)
            dve.wait_ge(x_rest, 16)
            ffn_tile(0, 0, 0, 1, first=True)
            dve.wait_ge(wa_in, 80)
            dve.wait_ge(wa_hi, 3)
            dve.scalar_tensor_tensor(out=WQ[:, 1, :, 0:D], in0=wqs[:, :, 0:D], scalar=0.25,
                                     in1=WQ[:, 0, :, 0:D].bitcast(F32), op0=ALU.mult, op1=ALU.subtract).then_inc(wa_lo, 1)
            dve.tensor_tensor(WQ[:, 1, :, D:3 * D], wqs[:, :, D:3 * D], WQ[:, 0, :, D:3 * D].bitcast(F32),
                              ALU.subtract).then_inc(wa_lo, 1)
            dve.tensor_tensor(WO[:, 1], wos[:], WO[:, 0].bitcast(F32), ALU.subtract).then_inc(wa_lo, 1)
            dve.tensor_scalar(bqk_s[:, 0:2], bqk_sb[:, 0:2], 0.25, None, ALU.mult).then_inc(wa_lo, 1)
            dve.tensor_copy(bqk_s[:, 2:4], bqk_sb[:, 2:4]).then_inc(wa_lo, 1)
            with dve.Fori(0, TILES - 1) as i:
                ffn_tile(1 + i, 1 + i, 1 + i, (i + 2) & (TILES - 1))

            def qk_low(c):
                for b in range(4):
                    dve.wait_ge(qk_hi, 4 * c + 2 * (b // 2) + 2)
                    dve.scalar_tensor_tensor(out=HL[:, b, 1, :], in0=ps[:, 6 + b // 2, S * (b % 2):S * (b % 2) + S],
                                             scalar=bqk_s[:, b:b + 1], in1=HL[:, b, 0, :].bitcast(F32),
                                             op0=ALU.add, op1=ALU.subtract).then_inc(qk_lo, 1)

            def v_add(c):
                dve.wait_ge(v_ready, c + 1)
                dve.wait_ge(v_3, c)
                dve.tensor_tensor(v32[:], ps[:, 6, :].rearrange("p (t d) -> p t d", t=2),
                                  bv_sb[:].unsqueeze(1).to_broadcast([P, 2, D]), ALU.add).then_inc(v_sum, 1)

            def maxima(c, p):
                hf, pp = p // HALF, p % HALF
                dve.wait_ge(s_ready, 8 * c + p + 1)
                dve.tensor_reduce(mx[:, hf, 1, :, pp], ps[:, 0:2, 0:256], AX.X, ALU.max)
                dve.tensor_reduce(mx[:, hf, 0, :, pp], ps[:, 0:2, 256:384], AX.X, ALU.max).then_inc(mx_done, 1)

            def neg_max(c, hf):
                k = 2 * c + hf
                dve.wait_ge(mx_done, 4 * k + 4)
                dve.wait_ge(mt_ready, k)
                m = mx[:, hf]
                nh, nl = NM[:, hf, :, :, 0, :], NM[:, hf, :, :, 1, :]
                dve.tensor_scalar(nh.bitcast(F32R), m, -1.0, None, ALU.mult).then_inc(nm_done, 1)
                dve.wait_ge(nm_done, 2 * k + 1)
                dve.scalar_tensor_tensor(out=nl.bitcast(F32R), in0=m, scalar=-1.0, in1=nh, op0=ALU.mult,
                                         op1=ALU.subtract).then_inc(nm_done, 1)

            def p_low(c, p):
                u = p % 2
                dve.wait_ge(exp_done, 16 * c + 2 * p + 2)
                if p >= 2:
                    dve.wait_ge(pv_done, 8 * c + p - 1)
                dve.tensor_tensor(Pl[:, u], Pf[:, u], Ph[:, u], ALU.subtract).then_inc(pl_done, 1)

            def context(c, hf):
                k = 2 * c + hf
                dve.wait_ge(pv_done, 4 * k + 4)
                dve.wait_ge(cx_done, k)
                for qt in range(2):
                    o = ps[:, 4 + qt, 0:8 * VP].rearrange("p (h v) -> p h v", v=VP)
                    dve.tensor_reduce(cs[:, qt], o[:, :, 0:3 * HD].rearrange("p h (t d) -> p h d t", t=3),
                                      AX.X, ALU.add).then_inc(red_done, 1)
                o = ps[:, 4:6, 0:8 * VP].rearrange("p q (h v) -> p q h v", v=VP)
                dve.reciprocal(rc[:], o[:, :, :, 3 * HD]).then_inc(rc_done, 1)
                dve.wait_ge(red_done, 2 * k + 2)
                dve.wait_ge(rc_done, k + 1)
                dve.wait_ge(ct_ready, c)
                dve.tensor_tensor(cx[:, :, P * hf:P * hf + P].rearrange("p q (h d) -> p q h d", h=8), cs[:],
                                  rc[:].unsqueeze(3).to_broadcast([P, 2, 8, HD]), ALU.mult).then_inc(cx_done, 1)

            def finish(c):
                dve.wait_ge(ct_hi, c + 1)
                dve.tensor_tensor(CT[:, 1], ps[:, 6, :].rearrange("p (k t) -> p k t", k=KT),
                                  CT[:, 0].bitcast(F32), ALU.subtract).then_inc(ct_lo, 1)
                xt = X[:, bass.ts(c, 2), :]
                dve.tensor_tensor(xt, xt, bo_sb[:].unsqueeze(1).to_broadcast([P, 2, D]), ALU.add).then_inc(xb_done, 1)
                dve.wait_ge(xb_done, c + 1)
                dve.wait_ge(o_ready, c + 1)
                dve.tensor_tensor(xt, xt, ps[:, 7, :].rearrange("p (t d) -> p t d", t=2), ALU.add).then_inc(ax_done, 1)

            with dve.Fori(0, TILES) as i:
                k = TILES + 1 + i
                nxt = (i + 1) & (TILES - 1)
                stats(k, nxt)
                normalise(k, nxt)
                for b in range(2):
                    c = 2 * i + b
                    qk_low(c)
                    v_add(c)
                    if b == 1:
                        y_low(k, (6, 7))
                    for p in range(PAIRS):
                        maxima(c, p)
                        if p % HALF == HALF - 1:
                            neg_max(c, p // HALF)
                    for p in range(PAIRS):
                        p_low(c, p)
                        if p == HALF:
                            context(c, 0)
                    context(c, 1)
                    finish(c)
            with dve.Fori(0, TILES) as i:
                ffn_tile(TILES + i, 2 * TILES + i, i, (i + 1) & (TILES - 1))

        @block.tensor
        def _(pe):
            def transpose_y(k, bank):
                pe.wait_ge(yn_done, SUB * (k + 1))
                for kt in range(KT):
                    for s in range(SUB):
                        mm = pe.transpose(ps[:, bank[kt], P * s:P * s + P], yn[:, s, kt::KT], ident[:, :])
                mm.then_inc(xt_done, 1)

            def product(out, w, col, rhs_h, rhs_l, start=True):
                for kt in range(KT):
                    for j, (a, b) in enumerate(((0, rhs_h), (1, rhs_h), (0, rhs_l))):
                        mm = pe.matmul(out, w[:, a, kt, col], b(kt), start=(kt == 0 and j == 0),
                                       stop=(kt == KT - 1 and j == 2))
                return mm

            def down(t, n, first):
                pe.wait_ge(hi_done, NT * t + n + 1)
                pe.wait_ge(lo_done, NT * t + n + 1)
                if n == 0 and not first:
                    pe.wait_ge(x_done, t)
                for s in range(SUB):
                    tok = slice(P * s, P * s + P)
                    pe.matmul(ps[:, s, :], ih[:, n % 3, tok], WD[:, n, :, :], start=(n == 0), stop=False,
                              skip_group_check=True)
                    mm = pe.matmul(ps[:, s, 0:D], il[:, n % 3, tok], WD[:, n, 0, :], start=False,
                                   stop=(n == NT - 1), skip_group_check=True)
                mm.then_inc(d_done, 1)

            def ffn_tile(t, k, first=False):
                pe.wait_ge(yh_done, KT * (k + 1))
                pe.wait_ge(yl_done, KT * (k + 1))
                yh, yl = (lambda kt: yT[:, 0, kt, :]), (lambda kt: yT[:, 1, kt, :])
                for n in range(NT):
                    col = slice(P * n, P * n + P)
                    if first and n % NCH == 0:
                        pe.wait_ge(w_lo, 6 * (n // NCH) + 2)
                    if n >= 2 or not first:
                        pe.wait_ge(gelu_done, NT * t + n - 1)
                    product(ps[:, 4 + n % 2, :], WG, col, yh, yl).then_inc(g_ready, 1)
                    if first and n % NCH == 0:
                        pe.wait_ge(w_lo, 6 * (n // NCH) + 4)
                    if n >= 2 or not first:
                        pe.wait_ge(inter_done, NT * t + n - 1)
                    product(ps[:, 6 + n % 2, :], WU, col, yh, yl).then_inc(u_ready, 1)
                    if n == NT - 1:
                        pe.wait_ge(gelu_done, NT * t + NT - 1)
                        pe.wait_ge(inter_done, NT * t + NT - 1)
                        transpose_y(k + 1, (4, 6))
                    if n >= 2:
                        if first and (n - 2) % NCH == 0:
                            pe.wait_ge(w_lo, 6 * ((n - 2) // NCH) + 6)
                        down(t, n - 2, first)
                down(t, NT - 2, first)
                down(t, NT - 1, first)

            pe.wait_ge(const_done, 4)
            transpose_y(0, (4, 6))
            ffn_tile(0, 0, first=True)
            with pe.Fori(0, TILES - 1) as i:
                ffn_tile(1 + i, 1 + i)

            pe.wait_ge(x_done, TILES)
            pe.wait_ge(wa_lo, 5)
            pe.wait_ge(gelu_done, NT * TILES)
            pe.wait_ge(inter_done, NT * TILES)

            def qk_project(c, b2):
                tok = slice(S * b2, S * b2 + S)
                pe.wait_ge(ct_lo, c)
                for b in range(4):
                    if b == 2:
                        pe.wait_ge(ax_done, c)
                    product(ps[:, 6 + b // 2, S * (b % 2):S * (b % 2) + S], WQ, slice(P * b, P * b + P),
                            lambda kt: yT[:, 0, kt, tok], lambda kt: yT[:, 1, kt, tok]).then_inc(qk_ready, 1)

            def v_project(c, b2):
                pe.wait_ge(qk_lo, 4 * c + 2)
                for t in range(2):
                    tok = slice(S * b2 + P * t, S * b2 + P * t + P)
                    for kt in range(KT):
                        for j, (a, w) in enumerate(((0, 0), (0, 1), (1, 0))):
                            mm = pe.matmul(ps[:, 6, D * t:D * t + D], yT[:, a, kt, tok], WQ[:, w, kt, 2 * D:3 * D],
                                           start=(kt == 0 and j == 0), stop=(kt == KT - 1 and j == 2))
                mm.then_inc(v_ready, 1)

            def scores(c, p):
                if p == 0:
                    pe.wait_ge(stk, 192 * (c + 1))
                pe.wait_ge(mx_done, 8 * c + p)
                for a in range(2):
                    r = slice(64 * a, 64 * a + 50)
                    pe.matmul(ps[:, a, 0:256], QS[r, p, P:2 * P], KS[r, p, 0:2 * P], start=True, stop=False,
                              skip_group_check=True)
                    pe.matmul(ps[:, a, 256:384], QS[r, p, 0:P], KS[r, p, 0:P], start=False, stop=False,
                              skip_group_check=True)
                for a in range(2):
                    mm = pe.matmul(ps[:, a, 128:384], identb[:, :], mask[:].rearrange("p a b -> p (a b)"), start=False,
                                   stop=True, skip_group_check=True)
                mm.then_inc(s_ready, 1)

            def transpose_max(c, hf):
                k = 2 * c + hf
                pe.wait_ge(nm_done, 2 * k + 2)
                pe.wait_ge(qk_lo, 4 * c + 4)
                pe.wait_ge(mt_copied, k)
                for qt in range(2):
                    mm = pe.transpose(ps[0:16, 7, P * qt:P * qt + P],
                                      NM[:, hf, qt].rearrange("p a l h -> p (a l h)"), ident[:, :])
                mm.then_inc(mt_ready, 1)

            def scores_t(c, p):
                if p % HALF == 0:
                    pe.wait_ge(m_rows[p // HALF], 64 * (c + 1))
                pe.wait_ge(exp_done, 16 * c + 2 * p)
                for a in range(2):
                    r = slice(64 * a, 64 * a + 52)
                    pe.matmul(ps[:, 2 + a, 128:384], KS[r, p, 0:P], QS[r, p, 0:2 * P], start=True, stop=False,
                              skip_group_check=True)
                    pe.matmul(ps[:, 2 + a, 0:128], KS[r, p, P:2 * P], QS[r, p, P:2 * P], start=False, stop=False,
                              skip_group_check=True)
                for a in range(2):
                    mm = pe.matmul(ps[:, 2 + a, 0:256], identb[:, :], maskT[:].rearrange("p a b -> p (a b)"), start=False,
                                   stop=True, skip_group_check=True)
                mm.then_inc(st_ready, 1)

            def values(c, p):
                if p == 0:
                    pe.wait_ge(v_3, c + 1)
                if p % HALF == 0:
                    pe.wait_ge(rc_done, 2 * c + p // HALF)
                pe.wait_ge(pl_done, 8 * c + p + 1)
                for a in range(2):
                    h = 2 * p + a
                    o = slice(VP * (h % 8), VP * (h % 8) + VP)
                    for qt, kt, col in ((0, 0, 128), (1, 0, 256), (1, 1, 0)):
                        for j, src in enumerate((Ph, Pl)):
                            mm = pe.matmul(ps[:, 4 + qt, o], src[:, p % 2, a, col:col + P], Vx[:, kt, h, 0:VP],
                                           start=(h % 8 == 0 and kt == 0 and j == 0), stop=(kt == qt and j == 1),
                                           skip_group_check=True)
                mm.then_inc(pv_done, 1)

            def transpose_ctx(c):
                pe.wait_ge(cx_done, 2 * c + 2)
                pe.wait_ge(v_sum, c + 1)
                for kt in range(KT):
                    for t in range(2):
                        mm = pe.transpose(ps[:, 6, S * kt + P * t:S * kt + P * t + P], cx[:, t, P * kt:P * kt + P],
                                          ident[:, :])
                mm.then_inc(ct_ready, 1)

            def out_project(c):
                pe.wait_ge(ct_lo, c + 1)
                pe.wait_ge(mt_copied, 2 * c + 2)
                for t in range(2):
                    for kt in range(KT):
                        for j, (a, w) in enumerate(((0, 0), (0, 1), (1, 0))):
                            mm = pe.matmul(ps[:, 7, D * t:D * t + D], CT[:, a, kt, P * t:P * t + P], WO[:, w, kt, :],
                                           start=(kt == 0 and j == 0), stop=(kt == KT - 1 and j == 2))
                mm.then_inc(o_ready, 1)

            pe.wait_ge(aux_st, 64)
            pe.wait_ge(vx_ones, 1)
            with pe.Fori(0, TILES) as i:
                pe.wait_ge(yh_done, KT * (TILES + 1 + i))
                pe.wait_ge(yl_done, KT * (TILES + 1 + i))
                for b in range(2):
                    c = 2 * i + b
                    qk_project(c, b)
                    v_project(c, b)
                    if b == 1:
                        pe.wait_ge(v_sum, c + 1)
                        pe.wait_ge(qk_lo, 4 * c + 4)
                        transpose_y(TILES + 1 + i, (6, 7))
                        pe.wait_ge(yl_done, KT * (TILES + 2 + i))
                    for p in range(PAIRS):
                        scores(c, p)
                        if p == HALF:
                            transpose_max(c, 0)
                    transpose_max(c, 1)
                    scores_t(c, 0)
                    for p in range(PAIRS):
                        if p + 1 < PAIRS:
                            scores_t(c, p + 1)
                        values(c, p)
                    transpose_ctx(c)
                    out_project(c)

            pe.wait_ge(ax_done, B)
            with pe.Fori(0, TILES) as i:
                ffn_tile(TILES + i, 2 * TILES + i)


def _bits12(v):
    b = v.astype(np.float32).view(np.uint32)
    return ((b + 0x7FF + ((b >> 12) & 1)) & np.uint32(0xFFFFF000)).view(np.float32)


def _stack_constants():
    pos = np.arange(1 - S, 1, dtype=np.float32)
    m = np.arange(1, H + 1, dtype=np.float32) * np.float32(8.0 / H)
    slopes = (np.float32(1.0) / np.float32(2.0) ** m).astype(np.float32)
    bias = (pos[None, :] * slopes[:, None]).astype(np.float32)
    hi = _bits12(bias)
    lo = bias - hi
    rows = np.ones((16, PAIRS, S), np.float32)
    for a in range(2):
        rows[4 * a] = hi[a::2]
        rows[4 * a + 1] = lo[a::2]
    return rows


def kernel(**inputs):
    import concourse.bacc as bacc
    from concourse.bass_utils import run_bass_kernel_spmd

    a = {k: np.asarray(v) for k, v in inputs.items()}
    cont = np.ascontiguousarray
    blk = MLP // (2 * P)

    def columns(w):
        return cont(w.T.reshape(w.shape[1], blk, P, 2).transpose(0, 1, 3, 2).reshape(w.shape[1], MLP))

    def spread(s):
        return cont(np.repeat(s, P // s.shape[0], axis=0))

    dpk = a["L0_ffn_down_W_packed"]
    dsc = a["L0_ffn_down_scales"]
    W = a["L0_attn_Wqkv"]
    bq = a["L0_attn_b_qkv"]

    def by_parity(m):
        return m.reshape(PAIRS, 2, HD, -1).transpose(1, 2, 0, 3).reshape(D, -1)

    Wr = np.concatenate([by_parity(W[0:D]), by_parity(W[D:2 * D]), W[2 * D:]])
    bqk = np.concatenate([by_parity(bq[0:D]), by_parity(bq[D:2 * D])]).reshape(4, P).T
    arrays = {
        "in_x": cont(a["L0_attn_x"]),
        "in_gate_pk": columns(a["L0_ffn_gate_W_packed"]),
        "in_gate_sc": spread(columns(a["L0_ffn_gate_scales"])),
        "in_up_pk": columns(a["L0_ffn_up_W_packed"]),
        "in_up_sc": spread(columns(a["L0_ffn_up_scales"])),
        "in_down_pk": cont(dpk.T.reshape(blk, P, D).transpose(1, 0, 2).reshape(P, MLP)),
        "in_down_sc": spread(cont(dsc.T.reshape(blk, 8, D).transpose(1, 0, 2).reshape(8, MLP))),
        "in_wqkv": cont(Wr.T.reshape(P, KT, 3 * D)),
        "in_bqk": cont(bqk),
        "in_bv": cont(bq[2 * D:]),
        "in_wout": cont(a["L0_attn_Wout"].T.reshape(KT, P, D).transpose(1, 0, 2)),
        "in_bout": cont(a["L0_attn_b_out"]),
        "in_aux": _stack_constants(),
    }
    nc = bacc.Bacc("TRN2", target_bir_lowering=False, num_devices=1)
    args = [nc.dram_tensor(n, v.shape, mybir.dt.from_np(v.dtype), kind="ExternalInput").ap()
            for n, v in arrays.items()]
    args.append(nc.dram_tensor("out_0", (B, S, D), F32, kind="ExternalOutput").ap())
    macaron_kernel(nc, *args)
    r = run_bass_kernel_spmd(nc, [arrays], core_ids=[0])
    return r.results[0]["out_0"]
```

```python
from contextlib import ExitStack

import numpy as np

import concourse.bass as bass
from concourse import mybir

F32, F32R, F16, BF16, I32 = (mybir.dt.float32, mybir.dt.float32r, mybir.dt.float16,
                             mybir.dt.bfloat16, mybir.dt.int32)
ALU = mybir.AluOpType
ACT = mybir.ActivationFunctionType
AX = mybir.AxisListType

P = 128
D = 256
KT = D // P
MLP = 2048
NT = MLP // P
B, S = 8, 256
TILE = 512
TILES = B * S // TILE
SUB = TILE // P
H, HD = 16, 16
PAIRS = H // 2
HALF = PAIRS // 2
CH = 512
CHUNKS = MLP // CH
NCH = CH // P
EPS = 1e-5
EXP_SHIFT = 15 * float(np.log(2.0))
MASKED = -1e30
VP = 3 * HD + 1
POOL_PAIRS = (1, 4, 6)
VW = 50
RING = 3


def macaron_kernel(nc, x, gate_pk, gate_sc, up_pk, up_sc, down_pk, down_sc, wqkv, bqk, bv, wout, bout, aux, out):
    ctx = ExitStack()
    with ctx:
        cursor = [nc.sbuf_base]

        def place(name, shape, dt, at=None):
            size = int(np.prod(shape[1:])) * (2 if dt in (F16, BF16) else 4)
            if at is None:
                at = (cursor[0] + 31) // 32 * 32
                cursor[0] = at + size
            return nc.alloc_sbuf_tensor_at(name, shape, dt, offset=at), at + size

        def sb(name, shape, dt):
            return place(name, shape, dt)[0]

        def sem(name):
            return ctx.enter_context(nc.semaphore(name))

        WG = sb("WG", [P, 2, KT, MLP], F32R)
        WU = sb("WU", [P, 2, KT, MLP], F32R)
        WD = sb("WD", [P, NT, 2, D], F32R)
        WQ = sb("WQ", [P, 2, KT, 3 * D], F32R)
        WO = sb("WO", [P, 2, KT, D], F32R)
        X = sb("X", [P, TILES * SUB, D], F32)
        yT = sb("yT", [P, 2, KT, TILE], F32R)
        yn = sb("yn", [P, SUB, D], F32)
        ident = sb("ident", [P, P], F32)
        identb = sb("identb", [P, P], BF16)
        mask = sb("mask", [P, 2, P], BF16)
        maskT = sb("maskT", [P, 2, P], BF16)
        bqk_sb = sb("bqk_sb", [P, 4], F32)
        bqk_s = sb("bqk_s", [P, 4], F32)
        bv_sb = sb("bv_sb", [P, D], F32)
        bo_sb = sb("bo_sb", [P, D], F32)
        st6 = sb("st6", [P, SUB, 6], F32)
        mv = sb("mv", [P, SUB, 2], F32)
        ve = sb("ve", [P, SUB], F32)
        rstd = sb("rstd", [P, SUB], F32)
        mhalf = sb("mhalf", [P, SUB], F32)
        epst = sb("epst", [P, SUB], F32)
        carry = sb("carry", [P, 1], F32)
        shift = sb("shift", [P, 1], F32)
        mx = sb("mx", [P, 2, 2, 2, HALF], F32)
        NM = sb("NM", [P, 2, 2, 2, 2, HALF], F32)
        rc = sb("rc", [P, 2, 8], F32)
        region = (cursor[0] + 31) // 32 * 32
        QS, e = place("QS", [P, 2, PAIRS, S], F32R, region)
        KS, region2 = place("KS", [P, 2, PAIRS, S], F32R, e)
        pk, e = place("pk", [P, 2, CH], I32, region)
        sc, e = place("sc", [P, 2, CH], F32, e)
        dT, e = place("dT", [P, 2, CH], I32, e)
        dU, e = place("dU", [P, 2, CH], I32, e)
        assert e <= region2
        ih, e = place("ih", [P, 3, TILE], F32R, region2)
        il, e = place("il", [P, 3, TILE], F32R, e)
        gb, e = place("gb", [P, 2, TILE], F32, e)
        tb, e = place("tb", [P, 2, TILE], F32, e)
        auxs, _ = place("auxs", [16, PAIRS, S], F32, e)
        auxr, _ = place("auxr", [16, PAIRS, S], F32R, e)
        wf, e = place("wf", [P, 2, CH], F32, e)
        wqs, e = place("wqs", [P, KT, 3 * D], F32, e)
        wos, e = place("wos", [P, KT, D], F32, e)
        end_a = e
        HL, e = place("HL", [P, 4, 2, S], F32R, region2)
        v32, e = place("v32", [P, 2, D], F32, e)
        vr, e = place("vr", [P, 2, D], F32, e)
        Vx, e = place("Vx", [P, 2, 2, H, VW], BF16, e)
        Pf, e = place("Pf", [P, 2, 2, 384], F32, e)
        Ph, e = place("Ph", [P, RING, 2, 384], F16, e)
        Pl, e = place("Pl", [P, RING, 2, 384], F16, e)
        cs, e = place("cs", [P, 2, 8, HD], F32, e)
        cx, e = place("cx", [P, 2, D], F32, e)
        CT, e = place("CT", [P, 2, KT, S], F32R, e)
        MT, e = place("MT", [16, 2, S], F32R, e)
        assert max(e, end_a) <= nc.sbuf_usable_end, (e, end_a, nc.sbuf_usable_end)

        ps = ctx.enter_context(nc.psum_tensor("ps", [P, 8, 512], F32))

        x_first = sem("x_first")
        x_rest = sem("x_rest")
        pk_in = [sem(f"pk_in{b}") for b in range(2)]
        sc_in = [sem(f"sc_in{b}") for b in range(2)]
        wa_in = sem("wa_in")
        const_done = sem("const_done")
        const_init = sem("const_init")
        vx_ones = sem("vx_ones")
        dec1 = sem("dec1")
        dec2 = sem("dec2")
        w_f = sem("w_f")
        w_hi = sem("w_hi")
        w_lo = sem("w_lo")
        wa_hi = sem("wa_hi")
        wa_lo = sem("wa_lo")
        bn1 = sem("bn1")
        bn2 = sem("bn2")
        ve_done = sem("ve_done")
        rstd_done = sem("rstd_done")
        yn_done = sem("yn_done")
        xt_done = sem("xt_done")
        yh_done = sem("yh_done")
        yl_done = sem("yl_done")
        g_ready = sem("g_ready")
        u_ready = sem("u_ready")
        gelu_done = sem("gelu_done")
        inter_done = sem("inter_done")
        hi_done = sem("hi_done")
        lo_done = sem("lo_done")
        d_done = sem("d_done")
        xa_done = sem("xa_done")
        x_done = sem("x_done")
        aux_in = sem("aux_in")
        aux_r = sem("aux_r")
        aux_st = sem("aux_st")
        qk_ready = sem("qk_ready")
        qk_hi = sem("qk_hi")
        qk_lo = sem("qk_lo")
        v_ready = sem("v_ready")
        v_sum = sem("v_sum")
        v_1 = sem("v_1")
        v_r = sem("v_r")
        v_2 = sem("v_2")
        v_3 = sem("v_3")
        stk = [[sem(f"stk{b}{h}") for h in range(2)] for b in range(2)]
        s_ready = sem("s_ready")
        mx_done = sem("mx_done")
        nm_done = sem("nm_done")
        mt_ready = sem("mt_ready")
        mt_copied = sem("mt_copied")
        m_rows = [[sem(f"m_rows{b}{h}") for h in range(2)] for b in range(2)]
        st_ready = sem("st_ready")
        exp_done = sem("exp_done")
        ph_done = sem("ph_done")
        pl_dve = sem("pl_dve")
        pl_pool = sem("pl_pool")
        pv_done = sem("pv_done")
        red_done = sem("red_done")
        rc_done = sem("rc_done")
        cx_done = sem("cx_done")
        ct_ready = sem("ct_ready")
        ct_hi = sem("ct_hi")
        ct_lo = sem("ct_lo")
        o_ready = sem("o_ready")
        xb_done = sem("xb_done")
        ax_done = sem("ax_done")
        stored = sem("stored")

        ROUNDS = [(w, c) for c in range(CHUNKS) for w in range(3)]

        def codes(w, c):
            return (gate_pk, up_pk, down_pk)[w][:, c * CH:(c + 1) * CH]

        def scales(w, c):
            return (gate_sc, up_sc, down_sc)[w][:, c * CH:(c + 1) * CH]

        def weights(w, c, par, part):
            if w < 2:
                return (WG, WU)[w][:, part, par, c * CH:(c + 1) * CH]
            return WD[:, 2 * (2 * c) + par:2 * (2 * c + 1) + par + 1:2, part, :]

        def split2(ap, w):
            return ap if w < 2 else ap.rearrange("p (j h) -> p j h", j=2)

        def wait_p_low(eng, c, u):
            if u in POOL_PAIRS:
                eng.wait_ge(pl_pool, len(POOL_PAIRS) * c + POOL_PAIRS.index(u) + 1)
            else:
                mine = [v for v in range(PAIRS) if v not in POOL_PAIRS]
                eng.wait_ge(pl_dve, len(mine) * c + mine.index(u) + 1)

        block = ctx.enter_context(nc.Block())

        @block.sync
        def _(sp):
            xv = x.rearrange("b (s p) d -> p (b s) d", p=P)
            ov = out.rearrange("b (s p) d -> p (b s) d", p=P)
            for r, (w, c) in enumerate(ROUNDS):
                if r >= 2:
                    sp.wait_ge(dec1, 2 * (r - 1))
                if r == 0:
                    sp.dma_start(X[:, 0:SUB, :], xv[:, 0:SUB, :]).then_inc(x_first, 16)
                sp.dma_start(pk[:, r % 2, :], codes(w, c)).then_inc(pk_in[r % 2], 16)
                if r >= 2:
                    sp.wait_ge(w_f, 2 * (r - 1))
                sp.dma_start(sc[:, r % 2, :], scales(w, c)).then_inc(sc_in[r % 2], 16)
                if r == 1:
                    sp.dma_start(X[:, SUB:, :], xv[:, SUB:, :]).then_inc(x_rest, 16)
            sp.dma_start(wqs[:], wqkv).then_inc(wa_in, 16)
            sp.dma_start(wos[:], wout).then_inc(wa_in, 16)
            sp.dma_start(bqk_sb[:], bqk).then_inc(wa_in, 16)
            sp.dma_start(bv_sb[:], bv.partition_broadcast(P)).then_inc(wa_in, 16)
            sp.dma_start(bo_sb[:], bout.partition_broadcast(P)).then_inc(wa_in, 16)
            sp.wait_ge(w_lo, 2 * len(ROUNDS))
            sp.wait_ge(wa_lo, 5)
            sp.dma_start(auxs[:], aux).then_inc(aux_in, 16)
            sp.wait_ge(aux_r, 1)
            for a in range(2):
                for b in range(2):
                    sp.dma_start(KS[64 * a + 48:64 * a + 52, b].bitcast(F32),
                                 auxr[4 * a:4 * a + 4].bitcast(F32)).then_inc(aux_st, 16)
                    sp.dma_start(QS[64 * a + 48:64 * a + 50, b].bitcast(F32),
                                 auxr[8 + 2 * a:10 + 2 * a].bitcast(F32)).then_inc(aux_st, 16)

            def stack_rows(c, b, hf):
                sp.wait_ge(qk_hi, 4 * c + 4)
                sp.wait_ge(qk_lo, 4 * c + 4)
                for t, dst in ((0, QS), (1, KS)):
                    for g, part in enumerate(((0, 0, 1), (0, 1, 0))[t]):
                        for a in range(2):
                            row = 64 * a + HD * g
                            sp.dma_start(dst[row:row + HD, b, HALF * hf:HALF * hf + HALF, :].bitcast(F32),
                                         HL[64 * hf:64 * hf + 64, 2 * t + a, part, :].bitcast(F32)
                                         ).then_inc(stk[b][hf], 16)

            def max_rows(c, b, hf):
                sp.wait_ge(mt_copied, 2 * c + hf + 1)
                for a in range(2):
                    for part in range(2):
                        r = 8 * a + 4 * part
                        sp.dma_start(QS[64 * a + 50 + part:64 * a + 51 + part, b, HALF * hf:HALF * hf + HALF, :]
                                     .bitcast(F32), MT[r:r + 4, hf, :].bitcast(F32)).then_inc(m_rows[b][hf], 16)

            def step(i, b, last):
                c = 2 * i + b
                for hf in range(2):
                    if not (last and b == 1):
                        max_rows(c + 1, 1 - b, hf)
                    if not last:
                        stack_rows(c + 2, b, hf)

            for c in range(2):
                for hf in range(2):
                    stack_rows(c, c, hf)
            for hf in range(2):
                max_rows(0, 0, hf)
            with sp.Fori(0, TILES - 1) as i:
                for b in range(2):
                    step(i, b, False)
            for b in range(2):
                step(TILES - 1, b, True)
            with sp.Fori(0, TILES) as i:
                first = sp.snap(SUB * i)
                sp.wait_ge(x_done, TILES + 1 + i)
                sp.dma_start(ov[:, bass.ds(first, SUB), :], X[:, bass.ds(first, SUB), :]).then_inc(stored, 16)
            sp.wait_ge(stored, 16 * TILES)

        @block.gpsimd
        def _(pool):
            for t, v in ((ident, 0.0), (identb, 0.0), (mask, 0.0), (maskT, 0.0), (mhalf, -0.5), (epst, EPS), (shift, EXP_SHIFT)):
                pool.memset(t[:], v).then_inc(const_init, 1)
            pool.wait_ge(const_init, 7)
            for t in (ident, identb):
                pool.affine_select(out=t[:, :], in_=t[:, :], compare_op=ALU.not_equal, fill=1.0, base=0,
                                   pattern=[[-1, P]], channel_multiplier=1).then_inc(const_done, 1)
            pool.affine_select(out=mask[:], in_=mask[:], compare_op=ALU.is_ge, fill=MASKED, base=0,
                               pattern=[[0, 2], [-1, P]], channel_multiplier=1).then_inc(const_done, 1)
            pool.affine_select(out=maskT[:], in_=maskT[:], compare_op=ALU.is_ge, fill=MASKED, base=0,
                               pattern=[[0, 2], [1, P]], channel_multiplier=-1).then_inc(const_done, 1)

            def inv_std(k):
                pool.wait_ge(bn2, SUB * (k + 1))
                pool.tensor_tensor(ve[:, :], mv[:, :, 1], epst[:, :], ALU.add).then_inc(ve_done, 1)
                pool.wait_ge(ve_done, k + 1)
                pool.tensor_tensor(rstd[:, :], ve[:, :], mhalf[:, :], ALU.pow).then_inc(rstd_done, 1)

            def w_low(r):
                w, c = ROUNDS[r]
                for par in range(2):
                    k = 2 * r + par
                    pool.wait_ge(w_hi, k + 1)
                    pool.tensor_tensor(weights(w, c, par, 1), split2(wf[:, par, :], w),
                                       weights(w, c, par, 0).bitcast(F32), ALU.subtract).then_inc(w_lo, 1)

            inv_std(0)
            for r in range(len(ROUNDS)):
                w_low(r)
                if r == 5:
                    inv_std(1)
            with pool.Fori(0, TILES - 1) as i:
                inv_std(2 + i)
            pool.wait_ge(x_done, TILES)
            pool.memset(Vx[:, :, :, :, 3 * HD], 1.0).then_inc(vx_ones, 1)

            def v_rest(c, b):
                if not (isinstance(c, int) and c == 0):
                    pool.wait_ge(v_3, c)
                pool.wait_ge(v_1, c + 1)
                pool.tensor_tensor(vr[:], v32[:], Vx[:, b, :, :, 0:HD], ALU.subtract).then_inc(v_r, 1)
                pool.wait_ge(v_2, c + 1)
                pool.tensor_tensor(Vx[:, b, :, :, 2 * HD:3 * HD], vr[:], Vx[:, b, :, :, HD:2 * HD],
                                   ALU.subtract).then_inc(v_3, 1)

            def p_low(c, u):
                pool.wait_ge(ph_done, 8 * c + u + 1)
                if u >= RING:
                    pool.wait_ge(pv_done, 8 * c + u - RING + 1)
                pool.tensor_tensor(Pl[:, u % RING], Pf[:, u % 2], Ph[:, u % RING], ALU.subtract).then_inc(pl_pool, 1)

            def step(i, b, last):
                c = 2 * i + b
                for u in POOL_PAIRS:
                    p_low(c, u)
                xt = X[:, bass.ts(c, 2), :]
                pool.tensor_tensor(xt, xt, bo_sb[:].unsqueeze(1).to_broadcast([P, 2, D]), ALU.add).then_inc(xb_done, 1)
                if not last:
                    v_rest(c + 2, b)
                if b == 1 and not last:
                    inv_std(TILES + 2 + i)

            for b in range(2):
                v_rest(b, b)
            inv_std(TILES + 1)
            with pool.Fori(0, TILES - 1) as i:
                for b in range(2):
                    step(i, b, False)
            for b in range(2):
                step(TILES - 1, b, True)
            with pool.Fori(0, TILES) as i:
                inv_std(2 * TILES + 1 + i)

        @block.scalar
        def _(act):
            def y_high(k, bank):
                act.wait_ge(xt_done, k + 1)
                for kt in range(KT):
                    act.activation(yT[:, 0, kt, :], ps[:, bank[kt], :], ACT.Copy).then_inc(yh_done, 1)

            def w_high(r):
                w, c = ROUNDS[r]
                for par in range(2):
                    k = 2 * r + par
                    act.wait_ge(w_f, k + 1)
                    act.activation(weights(w, c, par, 0), split2(wf[:, par, :], w), ACT.Copy).then_inc(w_hi, 1)

            def ffn_tile(t, k, first=False):
                for n in range(NT):
                    act.wait_ge(g_ready, NT * t + n + 1)
                    if n >= 2 or not first:
                        act.wait_ge(inter_done, NT * t + n - 1)
                    act.activation(gb[:, n % 2, :], ps[:, 4 + n % 2, :], ACT.Gelu_apprx_tanh).then_inc(gelu_done, 1)
                    act.wait_ge(inter_done, NT * t + n + 1)
                    if n == 0 and not first:
                        act.wait_ge(d_done, NT * t)
                    if n >= 3:
                        act.wait_ge(d_done, NT * t + n - 2)
                    act.activation(ih[:, n % 3, :], tb[:, n % 2, :], ACT.Copy).then_inc(hi_done, 1)
                    if first and n % NCH < 3 and n // NCH + 1 < CHUNKS:
                        w_high(3 * (n // NCH + 1) + n % NCH)
                y_high(k + 1, (4, 6))

            y_high(0, (4, 6))
            for w in range(3):
                w_high(w)
            ffn_tile(0, 0, first=True)
            act.wait_ge(wa_in, 80)
            act.activation(WQ[:, 0, :, 0:D], wqs[:, :, 0:D], ACT.Copy, scale=0.25).then_inc(wa_hi, 1)
            act.activation(WQ[:, 0, :, D:3 * D], wqs[:, :, D:3 * D], ACT.Copy).then_inc(wa_hi, 1)
            act.activation(WO[:, 0, :, :], wos[:], ACT.Copy).then_inc(wa_hi, 1)
            with act.Fori(0, TILES - 1) as i:
                ffn_tile(1 + i, 1 + i)

            act.wait_ge(aux_in, 16)
            act.activation(auxr[:], auxs[:], ACT.Copy).then_inc(aux_r, 1)

            def qk_high(c, t):
                for b in range(2 * t, 2 * t + 2):
                    act.wait_ge(qk_ready, 4 * c + 2 * t + 2)
                    act.activation(HL[:, b, 0, :], ps[:, 6 + t, S * (b % 2):S * (b % 2) + S], ACT.Identity,
                                   bias=bqk_s[:, b:b + 1]).then_inc(qk_hi, 1)

            def v_first(c, b):
                act.wait_ge(v_sum, c + 1)
                act.activation(Vx[:, b, :, :, 0:HD], v32[:].rearrange("p t (h d) -> p t h d", h=H),
                               ACT.Copy).then_inc(v_1, 1)

            def v_second(c, b):
                act.wait_ge(v_r, c + 1)
                act.activation(Vx[:, b, :, :, HD:2 * HD], vr[:].rearrange("p t (h d) -> p t h d", h=H),
                               ACT.Copy).then_inc(v_2, 1)

            def max_copy(c, hf):
                act.wait_ge(mt_ready, 2 * c + hf + 1)
                act.activation(MT[:, hf, :], ps[0:16, 7, 0:S], ACT.Copy).then_inc(mt_copied, 1)

            def exps(c, u):
                act.wait_ge(st_ready, 8 * c + u + 1)
                if u >= 2:
                    wait_p_low(act, c, u - 2)
                act.activation(Pf[:, u % 2], ps[:, 2:4, 0:384], ACT.Exp, bias=shift[:, 0:1]).then_inc(exp_done, 1)
                if u >= RING:
                    act.wait_ge(pv_done, 8 * c + u - RING + 1)
                act.wait_ge(exp_done, 8 * c + u + 1)
                act.activation(Ph[:, u % RING], Pf[:, u % 2], ACT.Copy).then_inc(ph_done, 1)

            def step(i, b, last):
                c = 2 * i + b
                more, qk = not (last and b == 1), not last
                exps(c, 1)
                if b == 0:
                    y_high(TILES + 1 + i, (6, 7))
                for u in range(2, 6):
                    exps(c, u)
                if qk:
                    for h in range(2):
                        act.wait_ge(stk[1 - b][h], 192 * (i + b + 1))
                    qk_high(c + 2, 0)
                exps(c, 6)
                if more:
                    act.wait_ge(m_rows[b][0], 64 * (i + 1))
                    max_copy(c + 1, 0)
                exps(c, 7)
                if qk:
                    qk_high(c + 2, 1)
                    v_first(c + 2, b)
                act.wait_ge(ct_ready, c + 1)
                act.activation(CT[:, 0], ps[:, 7, :].rearrange("p (k t) -> p k t", k=KT), ACT.Copy).then_inc(ct_hi, 1)
                if more:
                    exps(c + 1, 0)
                if qk:
                    v_second(c + 2, b)
                if more:
                    act.wait_ge(m_rows[b][1], 64 * (i + 1))
                    max_copy(c + 1, 1)

            for t in range(2):
                qk_high(0, t)
            v_first(0, 0)
            for h in range(2):
                act.wait_ge(stk[0][h], 192)
            qk_high(1, 0)
            v_second(0, 0)
            qk_high(1, 1)
            v_first(1, 1)
            v_second(1, 1)
            max_copy(0, 0)
            exps(0, 0)
            max_copy(0, 1)
            with act.Fori(0, TILES - 1) as i:
                for b in range(2):
                    step(i, b, False)
            for b in range(2):
                step(TILES - 1, b, True)
            with act.Fori(0, TILES) as i:
                ffn_tile(TILES + i, 2 * TILES + i)

        @block.vector
        def _(dve):
            def stats(k, tile):
                for s in range(SUB):
                    dve.bn_stats(st6[:, s, :], X[:, bass.ds(SUB * tile + s, 1), :].rearrange("p s d -> p (s d)")).then_inc(bn1, 1)
                dve.wait_ge(bn1, SUB * (k + 1))
                dve.memset(carry[:], 0.0)
                for s in range(SUB):
                    dve.bn_aggr(mv[:, s, :], st6[:, s, :]).then_inc(bn2, 1)

            def normalise(k, tile):
                dve.wait_ge(rstd_done, k + 1)
                if not (isinstance(k, int) and k == 0):
                    dve.wait_ge(xt_done, k)
                for s in range(SUB):
                    dve.tensor_scalar(yn[:, s, :], X[:, bass.ds(SUB * tile + s, 1), :].rearrange("p s d -> p (s d)"),
                                      mv[:, s, 0:1], rstd[:, s:s + 1], ALU.subtract, ALU.mult).then_inc(yn_done, 1)

            def y_low(k, bank):
                for kt in range(KT):
                    dve.wait_ge(yh_done, KT * k + kt + 1)
                    dve.tensor_tensor(yT[:, 1, kt, :], ps[:, bank[kt], :], yT[:, 0, kt, :].bitcast(F32),
                                      ALU.subtract).then_inc(yl_done, 1)

            def dequant(r):
                w, c = ROUNDS[r]
                u = r % 2
                dve.wait_ge(pk_in[u], 16 * (r // 2 + 1))
                for par in range(2):
                    dve.tensor_scalar(dT[:, par, :], pk[:, u, :], 28 - 4 * par, 19, ALU.logical_shift_left,
                                      ALU.arith_shift_right).then_inc(dec1, 1)
                for par in range(2):
                    dve.wait_ge(dec1, 2 * r + par + 1)
                    dve.tensor_scalar(dU[:, par, :], dT[:, par, :], 0x8E00, None, ALU.bitwise_and).then_inc(dec2, 1)
                dve.wait_ge(sc_in[u], 16 * (r // 2 + 1))
                for par in range(2):
                    dve.wait_ge(dec2, 2 * r + par + 1)
                    if r >= 1:
                        dve.wait_ge(w_lo, 2 * (r - 1) + par + 1)
                    dve.scalar_tensor_tensor(out=wf[:, par, :], in0=dU[:, par, :].bitcast(F16)[:, 0::2],
                                             scalar=float(2 ** 14), in1=sc[:, u, :], op0=ALU.mult,
                                             op1=ALU.mult).then_inc(w_f, 1)

            def ffn_tile(t, k, tile, nxt, first=False):
                for n in range(NT):
                    dve.wait_ge(u_ready, NT * t + n + 1)
                    dve.wait_ge(gelu_done, NT * t + n + 1)
                    if n >= 2 or not first:
                        dve.wait_ge(hi_done, NT * t + n - 1)
                        dve.wait_ge(lo_done, NT * t + n - 1)
                    dve.tensor_tensor(tb[:, n % 2, :], ps[:, 6 + n % 2, :], gb[:, n % 2, :],
                                      ALU.mult).then_inc(inter_done, 1)
                    dve.wait_ge(hi_done, NT * t + n + 1)
                    dve.tensor_tensor(il[:, n % 3, :], tb[:, n % 2, :], ih[:, n % 3, :].bitcast(F32),
                                      ALU.subtract).then_inc(lo_done, 1)
                    if n == 4:
                        stats(k + 1, nxt)
                    if n == 7:
                        normalise(k + 1, nxt)
                    if first and n % NCH < 3 and n // NCH + 1 < CHUNKS:
                        dequant(3 * (n // NCH + 1) + n % NCH)
                y_low(k + 1, (4, 6))
                dve.wait_ge(d_done, NT * (t + 1))
                xt = X[:, bass.ts(tile, SUB), :]
                dve.scalar_tensor_tensor(out=xt, in0=ps[:, 0:4, 0:D], scalar=0.5, in1=xt, op0=ALU.mult,
                                         op1=ALU.add).then_inc(xa_done, 1)
                dve.wait_ge(xa_done, t + 1)
                dve.scalar_tensor_tensor(out=xt, in0=ps[:, 0:4, D:2 * D], scalar=0.5, in1=xt, op0=ALU.mult,
                                         op1=ALU.add).then_inc(x_done, 1)

            dve.wait_ge(x_first, 16)
            stats(0, 0)
            dequant(0)
            normalise(0, 0)
            dequant(1)
            y_low(0, (4, 6))
            dequant(2)
            dve.wait_ge(x_rest, 16)
            ffn_tile(0, 0, 0, 1, first=True)
            dve.wait_ge(wa_in, 80)
            dve.wait_ge(wa_hi, 3)
            dve.scalar_tensor_tensor(out=WQ[:, 1, :, 0:D], in0=wqs[:, :, 0:D], scalar=0.25,
                                     in1=WQ[:, 0, :, 0:D].bitcast(F32), op0=ALU.mult, op1=ALU.subtract).then_inc(wa_lo, 1)
            dve.tensor_tensor(WQ[:, 1, :, D:3 * D], wqs[:, :, D:3 * D], WQ[:, 0, :, D:3 * D].bitcast(F32),
                              ALU.subtract).then_inc(wa_lo, 1)
            dve.tensor_tensor(WO[:, 1], wos[:], WO[:, 0].bitcast(F32), ALU.subtract).then_inc(wa_lo, 1)
            dve.tensor_scalar(bqk_s[:, 0:2], bqk_sb[:, 0:2], 0.25, None, ALU.mult).then_inc(wa_lo, 1)
            dve.tensor_copy(bqk_s[:, 2:4], bqk_sb[:, 2:4]).then_inc(wa_lo, 1)
            with dve.Fori(0, TILES - 1) as i:
                ffn_tile(1 + i, 1 + i, 1 + i, (i + 2) & (TILES - 1))

            def qk_low(c, t):
                for b in range(2 * t, 2 * t + 2):
                    dve.wait_ge(qk_hi, 4 * c + 2 * t + 2)
                    dve.scalar_tensor_tensor(out=HL[:, b, 1, :], in0=ps[:, 6 + t, S * (b % 2):S * (b % 2) + S],
                                             scalar=bqk_s[:, b:b + 1], in1=HL[:, b, 0, :].bitcast(F32),
                                             op0=ALU.add, op1=ALU.subtract).then_inc(qk_lo, 1)

            def v_add(c):
                if not (isinstance(c, int) and c == 0):
                    dve.wait_ge(v_r, c)
                dve.wait_ge(v_ready, c + 1)
                dve.tensor_tensor(v32[:], ps[:, 6, :].rearrange("p (t d) -> p t d", t=2),
                                  bv_sb[:].unsqueeze(1).to_broadcast([P, 2, D]), ALU.add).then_inc(v_sum, 1)

            def maxima(c, p):
                hf, pp = p // HALF, p % HALF
                dve.wait_ge(s_ready, 8 * c + p + 1)
                dve.tensor_reduce(mx[:, hf, 1, :, pp], ps[:, 0:2, 0:256], AX.X, ALU.max)
                dve.tensor_reduce(mx[:, hf, 0, :, pp], ps[:, 0:2, 256:384], AX.X, ALU.max).then_inc(mx_done, 1)

            def neg_max(c, hf):
                k = 2 * c + hf
                dve.wait_ge(mx_done, 4 * k + 4)
                m = mx[:, hf]
                nh, nl = NM[:, hf, :, :, 0, :], NM[:, hf, :, :, 1, :]
                dve.tensor_scalar(nh.bitcast(F32R), m, -1.0, None, ALU.mult).then_inc(nm_done, 1)
                dve.wait_ge(nm_done, 2 * k + 1)
                dve.scalar_tensor_tensor(out=nl.bitcast(F32R), in0=m, scalar=-1.0, in1=nh, op0=ALU.mult,
                                         op1=ALU.subtract).then_inc(nm_done, 1)

            def p_low(c, u):
                if u in POOL_PAIRS:
                    return
                dve.wait_ge(ph_done, 8 * c + u + 1)
                if u >= RING:
                    dve.wait_ge(pv_done, 8 * c + u - RING + 1)
                dve.tensor_tensor(Pl[:, u % RING], Pf[:, u % 2], Ph[:, u % RING], ALU.subtract).then_inc(pl_dve, 1)

            def context(c, hf):
                k = 2 * c + hf
                dve.wait_ge(pv_done, 4 * k + 4)
                for qt in range(2):
                    o = ps[:, 4 + qt, 0:8 * VP].rearrange("p (h v) -> p h v", v=VP)
                    dve.tensor_reduce(cs[:, qt], o[:, :, 0:3 * HD].rearrange("p h (t d) -> p h d t", t=3),
                                      AX.X, ALU.add).then_inc(red_done, 1)
                o = ps[:, 4:6, 0:8 * VP].rearrange("p q (h v) -> p q h v", v=VP)
                dve.reciprocal(rc[:], o[:, :, :, 3 * HD]).then_inc(rc_done, 1)
                dve.wait_ge(red_done, 2 * k + 2)
                dve.wait_ge(rc_done, k + 1)
                dve.tensor_tensor(cx[:, :, P * hf:P * hf + P].rearrange("p q (h d) -> p q h d", h=8), cs[:],
                                  rc[:].unsqueeze(3).to_broadcast([P, 2, 8, HD]), ALU.mult).then_inc(cx_done, 1)

            def step(i, b, last):
                c = 2 * i + b
                more, qk = not (last and b == 1), not last
                def a_unit(v):
                    if more:
                        maxima(c + 1, v)

                p_low(c, 0)
                a_unit(0)
                p_low(c, 1)
                if b == 0:
                    y_low(TILES + 1 + i, (6, 7))
                a_unit(1)
                p_low(c, 2)
                a_unit(2)
                p_low(c, 3)
                a_unit(3)
                if more:
                    neg_max(c + 1, 0)
                p_low(c, 4)
                context(c, 0)
                if qk:
                    qk_low(c + 2, 0)
                p_low(c, 5)
                a_unit(4)
                p_low(c, 6)
                a_unit(5)
                p_low(c, 7)
                if qk:
                    qk_low(c + 2, 1)
                a_unit(6)
                if b == 1 and not last:
                    stats(TILES + 2 + i, (i + 2) & (TILES - 1))
                context(c, 1)
                a_unit(7)
                if more:
                    neg_max(c + 1, 1)
                if qk:
                    v_add(c + 2)
                dve.wait_ge(ct_hi, c + 1)
                dve.tensor_tensor(CT[:, 1], ps[:, 7, :].rearrange("p (k t) -> p k t", k=KT),
                                  CT[:, 0].bitcast(F32), ALU.subtract).then_inc(ct_lo, 1)
                if b == 1 and not last:
                    normalise(TILES + 2 + i, (i + 2) & (TILES - 1))
                xt = X[:, bass.ts(c, 2), :]
                dve.wait_ge(xb_done, c + 1)
                dve.wait_ge(o_ready, c + 1)
                dve.tensor_tensor(xt, xt, ps[:, 6, :].rearrange("p (t d) -> p t d", t=2), ALU.add).then_inc(ax_done, 1)

            dve.sem_inc(ax_done, 1)
            for t in range(2):
                qk_low(0, t)
            v_add(0)
            for t in range(2):
                qk_low(1, t)
            v_add(1)
            for p in range(HALF):
                maxima(0, p)
            neg_max(0, 0)
            stats(TILES + 1, 1)
            for p in range(HALF, PAIRS):
                maxima(0, p)
            neg_max(0, 1)
            normalise(TILES + 1, 1)
            with dve.Fori(0, TILES - 1) as i:
                for b in range(2):
                    step(i, b, False)
            for b in range(2):
                step(TILES - 1, b, True)
            with dve.Fori(0, TILES) as i:
                ffn_tile(TILES + i, 2 * TILES + i, i, (i + 1) & (TILES - 1))

        @block.tensor
        def _(pe):
            def transpose_y(k, bank):
                pe.wait_ge(yn_done, SUB * (k + 1))
                for kt in range(KT):
                    for s in range(SUB):
                        mm = pe.transpose(ps[:, bank[kt], P * s:P * s + P], yn[:, s, kt::KT], ident[:, :])
                mm.then_inc(xt_done, 1)

            def product(out, w, col, rhs_h, rhs_l, start=True):
                for kt in range(KT):
                    for j, (a, b) in enumerate(((0, rhs_h), (1, rhs_h), (0, rhs_l))):
                        mm = pe.matmul(out, w[:, a, kt, col], b(kt), start=(kt == 0 and j == 0),
                                       stop=(kt == KT - 1 and j == 2))
                return mm

            def down(t, n, first):
                pe.wait_ge(hi_done, NT * t + n + 1)
                pe.wait_ge(lo_done, NT * t + n + 1)
                if n == 0 and not first:
                    pe.wait_ge(x_done, t)
                for s in range(SUB):
                    tok = slice(P * s, P * s + P)
                    pe.matmul(ps[:, s, :], ih[:, n % 3, tok], WD[:, n, :, :], start=(n == 0), stop=False,
                              skip_group_check=True)
                    mm = pe.matmul(ps[:, s, 0:D], il[:, n % 3, tok], WD[:, n, 0, :], start=False,
                                   stop=(n == NT - 1), skip_group_check=True)
                mm.then_inc(d_done, 1)

            def ffn_tile(t, k, first=False):
                pe.wait_ge(yh_done, KT * (k + 1))
                pe.wait_ge(yl_done, KT * (k + 1))
                yh, yl = (lambda kt: yT[:, 0, kt, :]), (lambda kt: yT[:, 1, kt, :])
                for n in range(NT):
                    col = slice(P * n, P * n + P)
                    if first and n % NCH == 0:
                        pe.wait_ge(w_lo, 6 * (n // NCH) + 2)
                    if n >= 2 or not first:
                        pe.wait_ge(gelu_done, NT * t + n - 1)
                    product(ps[:, 4 + n % 2, :], WG, col, yh, yl).then_inc(g_ready, 1)
                    if first and n % NCH == 0:
                        pe.wait_ge(w_lo, 6 * (n // NCH) + 4)
                    if n >= 2 or not first:
                        pe.wait_ge(inter_done, NT * t + n - 1)
                    product(ps[:, 6 + n % 2, :], WU, col, yh, yl).then_inc(u_ready, 1)
                    if n == NT - 1:
                        pe.wait_ge(gelu_done, NT * t + NT - 1)
                        pe.wait_ge(inter_done, NT * t + NT - 1)
                        transpose_y(k + 1, (4, 6))
                    if n >= 2:
                        if first and (n - 2) % NCH == 0:
                            pe.wait_ge(w_lo, 6 * ((n - 2) // NCH) + 6)
                        down(t, n - 2, first)
                down(t, NT - 2, first)
                down(t, NT - 1, first)

            pe.wait_ge(const_done, 4)
            transpose_y(0, (4, 6))
            ffn_tile(0, 0, first=True)
            with pe.Fori(0, TILES - 1) as i:
                ffn_tile(1 + i, 1 + i)

            pe.wait_ge(wa_lo, 5)
            pe.wait_ge(gelu_done, NT * TILES)
            pe.wait_ge(inter_done, NT * TILES)

            def qk_project(c, b, t):
                tok = slice(S * b, S * b + S)
                for a in range(2):
                    r = P * (2 * t + a)
                    product(ps[:, 6 + t, S * a:S * a + S], WQ, slice(r, r + P),
                            lambda kt: yT[:, 0, kt, tok], lambda kt: yT[:, 1, kt, tok]).then_inc(qk_ready, 1)

            def v_project(c, b):
                for t in range(2):
                    tok = slice(S * b + P * t, S * b + P * t + P)
                    for kt in range(KT):
                        for j, (a, w) in enumerate(((0, 0), (0, 1), (1, 0))):
                            mm = pe.matmul(ps[:, 6, D * t:D * t + D], yT[:, a, kt, tok], WQ[:, w, kt, 2 * D:3 * D],
                                           start=(kt == 0 and j == 0), stop=(kt == KT - 1 and j == 2))
                mm.then_inc(v_ready, 1)

            def scores(c, b, p, n):
                if p % HALF == 0:
                    pe.wait_ge(stk[b][p // HALF], 192 * n)
                if not (isinstance(c, int) and c == 0 and p == 0):
                    pe.wait_ge(mx_done, 8 * c + p)
                for a in range(2):
                    r = slice(64 * a, 64 * a + 50)
                    pe.matmul(ps[:, a, 0:256], QS[r, b, p, P:2 * P], KS[r, b, p, 0:2 * P], start=True, stop=False,
                              skip_group_check=True)
                    pe.matmul(ps[:, a, 256:384], QS[r, b, p, 0:P], KS[r, b, p, 0:P], start=False, stop=False,
                              skip_group_check=True)
                for a in range(2):
                    mm = pe.matmul(ps[:, a, 128:384], identb[:, :], mask[:].rearrange("p a b -> p (a b)"), start=False,
                                   stop=True, skip_group_check=True)
                mm.then_inc(s_ready, 1)

            def transpose_max(c, hf):
                k = 2 * c + hf
                bank = 7
                pe.wait_ge(nm_done, 2 * k + 2)
                for qt in range(2):
                    mm = pe.transpose(ps[0:16, bank, P * qt:P * qt + P],
                                      NM[:, hf, qt].rearrange("p a l h -> p (a l h)"), ident[:, :])
                mm.then_inc(mt_ready, 1)

            def scores_t(c, b, p, n):
                if p % HALF == 0:
                    pe.wait_ge(m_rows[b][p // HALF], 64 * n)
                if p >= 1:
                    pe.wait_ge(exp_done, 8 * c + p)
                for a in range(2):
                    r = slice(64 * a, 64 * a + 52)
                    pe.matmul(ps[:, 2 + a, 128:384], KS[r, b, p, 0:P], QS[r, b, p, 0:2 * P], start=True, stop=False,
                              skip_group_check=True)
                    pe.matmul(ps[:, 2 + a, 0:128], KS[r, b, p, P:2 * P], QS[r, b, p, P:2 * P], start=False, stop=False,
                              skip_group_check=True)
                for a in range(2):
                    mm = pe.matmul(ps[:, 2 + a, 0:256], identb[:, :], maskT[:].rearrange("p a b -> p (a b)"),
                                   start=False, stop=True, skip_group_check=True)
                mm.then_inc(st_ready, 1)

            def values(c, b, p):
                if p == 0:
                    pe.wait_ge(v_3, c + 1)
                if p == HALF:
                    pe.wait_ge(rc_done, 2 * c + 1)
                    pe.wait_ge(red_done, 4 * c + 2)
                wait_p_low(pe, c, p)
                for a in range(2):
                    h = 2 * p + a
                    o = slice(VP * (h % 8), VP * (h % 8) + VP)
                    for qt, kt, col in ((0, 0, 128), (1, 0, 256), (1, 1, 0)):
                        for j, src in enumerate((Ph, Pl)):
                            mm = pe.matmul(ps[:, 4 + qt, o], src[:, p % RING, a, col:col + P], Vx[:, b, kt, h, 0:VP],
                                           start=(h % 8 == 0 and kt == 0 and j == 0), stop=(kt == qt and j == 1),
                                           skip_group_check=True)
                mm.then_inc(pv_done, 1)

            def transpose_ctx(c):
                pe.wait_ge(cx_done, 2 * c + 2)
                for kt in range(KT):
                    for t in range(2):
                        mm = pe.transpose(ps[:, 7, S * kt + P * t:S * kt + P * t + P], cx[:, t, P * kt:P * kt + P],
                                          ident[:, :])
                mm.then_inc(ct_ready, 1)

            def out_project(c):
                pe.wait_ge(ct_lo, c + 1)
                for t in range(2):
                    for kt in range(KT):
                        for j, (a, w) in enumerate(((0, 0), (0, 1), (1, 0))):
                            mm = pe.matmul(ps[:, 6, D * t:D * t + D], CT[:, a, kt, P * t:P * t + P], WO[:, w, kt, :],
                                           start=(kt == 0 and j == 0), stop=(kt == KT - 1 and j == 2))
                mm.then_inc(o_ready, 1)

            def step(i, b, last):
                c = 2 * i + b
                more, qk = not (last and b == 1), not last

                def a_unit(v):
                    if more:
                        scores(c + 1, 1 - b, v, i + b + 1)

                scores_t(c, b, 1, i + 1)
                a_unit(0)
                if b == 0:
                    pe.wait_ge(mt_copied, 2 * c + 2)
                    pe.wait_ge(ax_done, c + 1)
                    transpose_y(TILES + 1 + i, (6, 7))
                scores_t(c, b, 2, i + 1)
                values(c, b, 0)
                a_unit(1)
                scores_t(c, b, 3, i + 1)
                values(c, b, 1)
                a_unit(2)
                scores_t(c, b, 4, i + 1)
                values(c, b, 2)
                a_unit(3)
                scores_t(c, b, 5, i + 1)
                values(c, b, 3)
                if qk:
                    pe.wait_ge(yh_done, KT * (TILES + 2 + i))
                    pe.wait_ge(yl_done, KT * (TILES + 2 + i))
                    pe.wait_ge(ax_done, c + 1)
                    qk_project(c + 2, b, 0)
                scores_t(c, b, 6, i + 1)
                a_unit(4)
                values(c, b, 4)
                if more:
                    if b == 0:
                        pe.wait_ge(yl_done, KT * (TILES + 2 + i))
                    else:
                        pe.wait_ge(mt_copied, 2 * c + 2)
                    transpose_max(c + 1, 0)
                scores_t(c, b, 7, i + 1)
                values(c, b, 5)
                a_unit(5)
                if more:
                    pe.wait_ge(mt_copied, 2 * c + 3)
                if qk:
                    qk_project(c + 2, b, 1)
                values(c, b, 6)
                a_unit(6)
                values(c, b, 7)
                if qk:
                    pe.wait_ge(qk_lo, 4 * c + 10)
                    v_project(c + 2, b)
                a_unit(7)
                if qk:
                    pe.wait_ge(qk_lo, 4 * c + 12)
                elif not more:
                    pe.wait_ge(mt_copied, 2 * c + 2)
                transpose_ctx(c)
                if more:
                    scores_t(c + 1, 1 - b, 0, i + b + 1)
                if qk:
                    pe.wait_ge(v_sum, c + 3)
                elif b == 0:
                    pe.wait_ge(yl_done, KT * (TILES + 2 + i))
                else:
                    pe.wait_ge(ax_done, c + 1)
                out_project(c)
                if more:
                    transpose_max(c + 1, 1)

            pe.wait_ge(yh_done, KT * (TILES + 1))
            pe.wait_ge(yl_done, KT * (TILES + 1))
            for t in range(2):
                qk_project(0, 0, t)
            pe.wait_ge(qk_lo, 2)
            v_project(0, 0)
            pe.wait_ge(v_sum, 1)
            qk_project(1, 1, 0)
            pe.wait_ge(qk_lo, 4)
            qk_project(1, 1, 1)
            pe.wait_ge(qk_lo, 6)
            v_project(1, 1)
            pe.wait_ge(x_done, TILES)
            pe.wait_ge(aux_st, 128)
            for p in range(HALF):
                scores(0, 0, p, 1)
            pe.wait_ge(qk_lo, 8)
            transpose_max(0, 0)
            scores(0, 0, HALF, 1)
            scores(0, 0, HALF + 1, 1)
            scores_t(0, 0, 0, 1)
            scores(0, 0, HALF + 2, 1)
            scores(0, 0, HALF + 3, 1)
            pe.wait_ge(mt_copied, 1)
            transpose_max(0, 1)
            pe.wait_ge(v_sum, 2)
            pe.wait_ge(vx_ones, 1)
            with pe.Fori(0, TILES - 1) as i:
                for b in range(2):
                    step(i, b, False)
            for b in range(2):
                step(TILES - 1, b, True)

            pe.wait_ge(ax_done, B + 1)
            with pe.Fori(0, TILES) as i:
                ffn_tile(TILES + i, 2 * TILES + i)


def _bits12(v):
    b = v.astype(np.float32).view(np.uint32)
    return ((b + 0x7FF + ((b >> 12) & 1)) & np.uint32(0xFFFFF000)).view(np.float32)


def _stack_constants():
    pos = np.arange(1 - S, 1, dtype=np.float32)
    m = np.arange(1, H + 1, dtype=np.float32) * np.float32(8.0 / H)
    slopes = (np.float32(1.0) / np.float32(2.0) ** m).astype(np.float32)
    bias = (pos[None, :] * slopes[:, None]).astype(np.float32)
    hi = _bits12(bias)
    lo = bias - hi
    rows = np.ones((16, PAIRS, S), np.float32)
    for a in range(2):
        rows[4 * a] = hi[a::2]
        rows[4 * a + 1] = lo[a::2]
    return rows


def kernel(**inputs):
    import concourse.bacc as bacc
    from concourse.bass_utils import run_bass_kernel_spmd

    a = {k: np.asarray(v) for k, v in inputs.items()}
    cont = np.ascontiguousarray
    blk = MLP // (2 * P)

    def columns(w):
        return cont(w.T.reshape(w.shape[1], blk, P, 2).transpose(0, 1, 3, 2).reshape(w.shape[1], MLP))

    def spread(s):
        return cont(np.repeat(s, P // s.shape[0], axis=0))

    dpk = a["L0_ffn_down_W_packed"]
    dsc = a["L0_ffn_down_scales"]
    W = a["L0_attn_Wqkv"]
    bq = a["L0_attn_b_qkv"]

    def by_parity(m):
        return m.reshape(2, HALF, 2, HD, -1).transpose(2, 0, 3, 1, 4).reshape(D, -1)

    Wr = np.concatenate([by_parity(W[0:D]), by_parity(W[D:2 * D]), W[2 * D:]])
    bqk = np.concatenate([by_parity(bq[0:D]), by_parity(bq[D:2 * D])]).reshape(4, P).T
    arrays = {
        "in_x": cont(a["L0_attn_x"]),
        "in_gate_pk": columns(a["L0_ffn_gate_W_packed"]),
        "in_gate_sc": spread(columns(a["L0_ffn_gate_scales"])),
        "in_up_pk": columns(a["L0_ffn_up_W_packed"]),
        "in_up_sc": spread(columns(a["L0_ffn_up_scales"])),
        "in_down_pk": cont(dpk.T.reshape(blk, P, D).transpose(1, 0, 2).reshape(P, MLP)),
        "in_down_sc": spread(cont(dsc.T.reshape(blk, 8, D).transpose(1, 0, 2).reshape(8, MLP))),
        "in_wqkv": cont(Wr.T.reshape(P, KT, 3 * D)),
        "in_bqk": cont(bqk),
        "in_bv": cont(bq[2 * D:]),
        "in_wout": cont(a["L0_attn_Wout"].T.reshape(KT, P, D).transpose(1, 0, 2)),
        "in_bout": cont(a["L0_attn_b_out"]),
        "in_aux": _stack_constants(),
    }
    nc = bacc.Bacc("TRN2", target_bir_lowering=False, num_devices=1, dynamic_dma_scratch_size=4096)
    args = [nc.dram_tensor(n, v.shape, mybir.dt.from_np(v.dtype), kind="ExternalInput").ap()
            for n, v in arrays.items()]
    args.append(nc.dram_tensor("out_0", (B, S, D), F32, kind="ExternalOutput").ap())
    macaron_kernel(nc, *args)
    r = run_bass_kernel_spmd(nc, [arrays], core_ids=[0])
    return r.results[0]["out_0"]
```

```python
from contextlib import ExitStack

import numpy as np

import concourse.bass as bass
from concourse import mybir

F32, F32R, F16, BF16, I32 = (mybir.dt.float32, mybir.dt.float32r, mybir.dt.float16,
                             mybir.dt.bfloat16, mybir.dt.int32)
ALU = mybir.AluOpType
ACT = mybir.ActivationFunctionType
AX = mybir.AxisListType

P = 128
D = 256
KT = D // P
MLP = 2048
NT = MLP // P
B, S = 8, 256
TILE = 512
TILES = B * S // TILE
SUB = TILE // P
H, HD = 16, 16
PAIRS = H // 2
HALF = PAIRS // 2
CH = 512
CHUNKS = MLP // CH
NCH = CH // P
EPS = 1e-5
EXP_SHIFT = 15 * float(np.log(2.0))
MASKED = -1e30
VP = 3 * HD + 1
POOL_PAIRS = (0, 2, 5, 6)
VW = VP + 1
RING = 3


def macaron_kernel(nc, x, gate_pk, gate_sc, up_pk, up_sc, down_pk, down_sc, wqkv, bqk, bv, wout, bout, aux, out):
    ctx = ExitStack()
    with ctx:
        cursor = [nc.sbuf_base]

        def place(name, shape, dt, at=None):
            size = int(np.prod(shape[1:])) * (2 if dt in (F16, BF16) else 4)
            if at is None:
                at = (cursor[0] + 31) // 32 * 32
                cursor[0] = at + size
            return nc.alloc_sbuf_tensor_at(name, shape, dt, offset=at), at + size

        def sb(name, shape, dt):
            return place(name, shape, dt)[0]

        def sem(name):
            return ctx.enter_context(nc.semaphore(name))

        WG = sb("WG", [P, 2, KT, MLP], F32R)
        WU = sb("WU", [P, 2, KT, MLP], F32R)
        WD = sb("WD", [P, NT, 2, D], F32R)
        WQ = sb("WQ", [P, 2, KT, 3 * D], F32R)
        WO = sb("WO", [P, 2, KT, D], F32R)
        X = sb("X", [P, TILES * SUB, D], F32)
        yT = sb("yT", [P, 2, KT, TILE], F32R)
        yn = sb("yn", [P, SUB, D], F32)
        ident = sb("ident", [P, P], F32)
        identb = sb("identb", [P, P], BF16)
        mask = sb("mask", [P, 2, P], BF16)
        maskT = sb("maskT", [P, 2, P], BF16)
        bqk_sb = sb("bqk_sb", [P, 4], F32)
        bqk_s = sb("bqk_s", [P, 4], F32)
        bv_sb = sb("bv_sb", [P, D], F32)
        bo_sb = sb("bo_sb", [P, D], F32)
        st6 = sb("st6", [P, SUB, 6], F32)
        mv = sb("mv", [P, SUB, 2], F32)
        ve = sb("ve", [P, SUB], F32)
        rstd = sb("rstd", [P, SUB], F32)
        mhalf = sb("mhalf", [P, SUB], F32)
        epst = sb("epst", [P, SUB], F32)
        carry = sb("carry", [P, 1], F32)
        shift = sb("shift", [P, 1], F32)
        mx = sb("mx", [P, 2, 2, 2, HALF], F32)
        NM = sb("NM", [P, 2, 2, 2, 2, HALF], F32)
        rc = sb("rc", [P, 2, 8], F32)
        region = (cursor[0] + 31) // 32 * 32
        QS, e = place("QS", [P, 2, PAIRS, S], F32R, region)
        auxs, _ = place("auxs", [16, PAIRS, S], F32, e)
        auxr, _ = place("auxr", [16, PAIRS, S], F32R, e)
        KS, region2 = place("KS", [P, 2, PAIRS, S], F32R, e)
        pk, e = place("pk", [P, 2, CH], I32, region)
        sc, e = place("sc", [P, 2, CH], F32, e)
        dT, e = place("dT", [P, 2, CH], I32, e)
        dU, e = place("dU", [P, 2, CH], I32, e)
        assert e <= region2
        ih, e = place("ih", [P, 3, TILE], F32R, region2)
        il, e = place("il", [P, 3, TILE], F32R, e)
        gb, e = place("gb", [P, 2, TILE], F32, e)
        tb, e = place("tb", [P, 2, TILE], F32, e)
        wf, e = place("wf", [P, 2, 2, CH], F32, e)
        wqs, e = place("wqs", [P, KT, 3 * D], F32, e)
        wos, e = place("wos", [P, KT, D], F32, e)
        end_a = e
        assert e <= nc.sbuf_usable_end
        HL, e = place("HL", [P, 4, 2, S], F32R, region2)
        v32, e = place("v32", [P, 2, D], F32, e)
        Vx, e = place("Vx", [P, 2, 2, H, VW], BF16, e)
        Pf, e = place("Pf", [P, RING, 2, 384], F32, e)
        Ph, e = place("Ph", [P, RING, 2, 384], F16, e)
        Pl, e = place("Pl", [P, RING, 2, 384], F16, e)
        HL1, e1 = place("HL1", [P, 4, 2, S], F32R, e)
        cs, e = place("cs", [P, 2, 8, HD], F32, e)
        cx, e = place("cx", [P, 2, D], F32, e)
        CT, e = place("CT", [P, 2, KT, S], F32R, e)
        MT, e = place("MT", [16, S], F32R, max(e, e1))
        assert max(e, end_a) <= nc.sbuf_usable_end, (e, end_a, nc.sbuf_usable_end)

        ps = ctx.enter_context(nc.psum_tensor("ps", [P, 8, 512], F32))

        x_first = [sem(f"x_first{h}") for h in range(2)]
        x_rest = sem("x_rest")
        pk_in = [sem(f"pk_in{b}") for b in range(2)]
        sc_in = [sem(f"sc_in{b}") for b in range(2)]
        wa_in = sem("wa_in")
        const_done = sem("const_done")
        const_init = sem("const_init")
        vx_ones = sem("vx_ones")
        dec1 = sem("dec1")
        dec2 = sem("dec2")
        w_f = sem("w_f")
        w_hi = sem("w_hi")
        w_lo = sem("w_lo")
        wa_hi = sem("wa_hi")
        wa_lo = sem("wa_lo")
        bn1 = sem("bn1")
        bn2 = sem("bn2")
        ve_done = sem("ve_done")
        rstd_done = sem("rstd_done")
        yn_done = sem("yn_done")
        xt_done = sem("xt_done")
        yh_done = sem("yh_done")
        yl_done = sem("yl_done")
        g_ready = sem("g_ready")
        u_ready = sem("u_ready")
        gelu_done = sem("gelu_done")
        inter_done = sem("inter_done")
        hi_done = sem("hi_done")
        lo_done = sem("lo_done")
        d_done = sem("d_done")
        xa_done = sem("xa_done")
        x_done = sem("x_done")
        aux_in = sem("aux_in")
        aux_r = sem("aux_r")
        aux_st = sem("aux_st")
        qk_ready = sem("qk_ready")
        qk_hi = sem("qk_hi")
        qk_lo = sem("qk_lo")
        v_ready = sem("v_ready")
        v_sum = sem("v_sum")
        v_1 = sem("v_1")
        v_r = sem("v_r")
        v_2 = sem("v_2")
        v_3 = sem("v_3")
        stk = [sem(f"stk{b}") for b in range(2)]
        s_ready = sem("s_ready")
        mx_done = sem("mx_done")
        nm_done = sem("nm_done")
        mt_ready = sem("mt_ready")
        mt_copied = sem("mt_copied")
        m_rows = [[sem(f"m_rows{b}{h}") for h in range(2)] for b in range(2)]
        st_ready = sem("st_ready")
        exp_done = sem("exp_done")
        ph_done = sem("ph_done")
        pl_dve = sem("pl_dve")
        pl_pool = sem("pl_pool")
        pv_done = sem("pv_done")
        red_done = sem("red_done")
        rc_done = sem("rc_done")
        cx_done = sem("cx_done")
        ct_ready = sem("ct_ready")
        ct_hi = sem("ct_hi")
        ct_lo = sem("ct_lo")
        o_ready = sem("o_ready")
        xb_done = sem("xb_done")
        ax_done = sem("ax_done")
        stored = sem("stored")

        ROUNDS = [(w, c) for c in range(CHUNKS) for w in range(3)]
        ROUND_AT = {0: 3, 1: 4, 3: 5, 4: 6, 6: 7, 7: 8, 8: 9, 10: 10, 11: 11}

        def codes(w, c):
            return (gate_pk, up_pk, down_pk)[w][:, c * CH:(c + 1) * CH]

        def scales(w, c):
            return (gate_sc, up_sc, down_sc)[w][:, c * CH:(c + 1) * CH]

        def weights(w, c, par, part):
            if w < 2:
                return (WG, WU)[w][:, part, par, c * CH:(c + 1) * CH]
            return WD[:, 2 * (2 * c) + par:2 * (2 * c + 1) + par + 1:2, part, :]

        def split2(ap, w):
            return ap if w < 2 else ap.rearrange("p (j h) -> p j h", j=2)

        def wait_p_low(eng, c, u):
            if u in POOL_PAIRS:
                eng.wait_ge(pl_pool, len(POOL_PAIRS) * c + POOL_PAIRS.index(u) + 1)
            else:
                mine = [v for v in range(PAIRS) if v not in POOL_PAIRS]
                eng.wait_ge(pl_dve, len(mine) * c + mine.index(u) + 1)

        def st_bank(c, u):
            return 0 if isinstance(c, int) and c == B - 1 and u >= 2 and u % 2 == 0 else 2

        def out_bank(c):
            return 0 if isinstance(c, int) and c == B - 1 else 6

        block = ctx.enter_context(nc.Block())

        @block.sync
        def _(sp):
            xv = x.rearrange("b (s p) d -> p (b s) d", p=P)
            ov = out.rearrange("b (s p) d -> p (b s) d", p=P)
            for r, (w, c) in enumerate(ROUNDS):
                if r >= 2:
                    sp.wait_ge(dec1, 2 * (r - 1))
                if r == 0:
                    for h in range(2):
                        sp.dma_start(X[:, 2 * h:2 * h + 2, :], xv[:, 2 * h:2 * h + 2, :]).then_inc(x_first[h], 16)
                sp.dma_start(pk[:, r % 2, :], codes(w, c)).then_inc(pk_in[r % 2], 16)
                if r >= 2:
                    sp.wait_ge(w_f, 2 * (r - 1))
                sp.dma_start(sc[:, r % 2, :], scales(w, c)).then_inc(sc_in[r % 2], 16)
                if r == 1:
                    sp.dma_start(X[:, SUB:, :], xv[:, SUB:, :]).then_inc(x_rest, 16)
            sp.dma_start(wqs[:], wqkv).then_inc(wa_in, 16)
            sp.dma_start(wos[:], wout).then_inc(wa_in, 16)
            sp.dma_start(bqk_sb[:], bqk).then_inc(wa_in, 16)
            sp.dma_start(bv_sb[:], bv.partition_broadcast(P)).then_inc(wa_in, 16)
            sp.dma_start(bo_sb[:], bout.partition_broadcast(P)).then_inc(wa_in, 16)
            sp.dma_start(auxs[:], aux).then_inc(aux_in, 16)
            sp.wait_ge(w_f, 2 * len(ROUNDS))
            sp.wait_ge(aux_r, 1)
            for a in range(2):
                for b in range(2):
                    sp.dma_start(KS[64 * a + 48:64 * a + 52, b].bitcast(F32),
                                 auxr[4 * a:4 * a + 4].bitcast(F32)).then_inc(aux_st, 16)
                    sp.dma_start(QS[64 * a + 48:64 * a + 50, b].bitcast(F32),
                                 auxr[8 + 2 * a:10 + 2 * a].bitcast(F32)).then_inc(aux_st, 16)

            def stack_rows(c, b, src, tensors=(0, 1)):
                for part, done in ((0, qk_hi), (1, qk_lo)):
                    for t in tensors:
                        sp.wait_ge(done, 4 * c + 2 * t + 2)
                        for g, which in enumerate(((0, 0, 1), (0, 1, 0))[t]):
                            for a in range(2):
                                if which == part:
                                    row = 64 * a + HD * g
                                    sp.dma_start((QS, KS)[t][row:row + HD, b].bitcast(F32),
                                                 src[:, 2 * t + a, part, :].bitcast(F32)).then_inc(stk[b], 16)

            def max_rows(c, b, hf):
                sp.wait_ge(mt_copied, 2 * c + hf + 1)
                for a in range(2):
                    sp.dma_start(QS[64 * a + 50:64 * a + 52, b, HALF * hf:HALF * hf + HALF, :].bitcast(F32),
                                 MT[8 * a:8 * a + 8, :].bitcast(F32)).then_inc(m_rows[b][hf], 16)

            def step(i, b, last):
                c = 2 * i + b
                if not (last and b == 1):
                    max_rows(c + 1, 1 - b, 0)
                if not last:
                    sp.wait_ge(st_ready, 8 * c + 8)
                    stack_rows(c + 2, b, HL)
                if not (last and b == 1):
                    max_rows(c + 1, 1 - b, 1)

            sp.wait_ge(aux_st, 128)
            stack_rows(0, 0, HL)
            stack_rows(1, 1, HL1, (0,))
            max_rows(0, 0, 0)
            stack_rows(1, 1, HL1, (1,))
            max_rows(0, 0, 1)
            with sp.Fori(0, TILES - 1) as i:
                for b in range(2):
                    step(i, b, False)
            for b in range(2):
                step(TILES - 1, b, True)
            with sp.Fori(0, TILES) as i:
                half = [sp.snap(SUB * i), sp.snap(SUB * i + 2)]
                for h in range(2):
                    sp.wait_ge(x_done, 2 * (TILES + i) + h + 1)
                    sp.dma_start(ov[:, bass.ds(half[h], 2), :], X[:, bass.ds(half[h], 2), :]).then_inc(stored, 16)
            sp.wait_ge(stored, 2 * 16 * TILES)

        @block.gpsimd
        def _(pool):
            for t, v in ((ident, 0.0), (identb, 0.0), (mask, 0.0), (maskT, 0.0), (mhalf, -0.5), (epst, EPS), (shift, EXP_SHIFT)):
                pool.memset(t[:], v).then_inc(const_init, 1)
            pool.wait_ge(const_init, 7)
            for t in (ident, identb):
                pool.affine_select(out=t[:, :], in_=t[:, :], compare_op=ALU.not_equal, fill=1.0, base=0,
                                   pattern=[[-1, P]], channel_multiplier=1).then_inc(const_done, 1)
            pool.affine_select(out=mask[:], in_=mask[:], compare_op=ALU.is_ge, fill=MASKED, base=0,
                               pattern=[[0, 2], [-1, P]], channel_multiplier=1).then_inc(const_done, 1)
            pool.affine_select(out=maskT[:], in_=maskT[:], compare_op=ALU.is_ge, fill=MASKED, base=0,
                               pattern=[[0, 2], [1, P]], channel_multiplier=-1).then_inc(const_done, 1)

            def inv_std(k):
                pool.wait_ge(bn2, SUB * (k + 1))
                pool.tensor_tensor(ve[:, :], mv[:, :, 1], epst[:, :], ALU.add).then_inc(ve_done, 1)
                pool.wait_ge(ve_done, k + 1)
                pool.tensor_tensor(rstd[:, :], ve[:, :], mhalf[:, :], ALU.pow).then_inc(rstd_done, 1)

            def w_low(r):
                w, c = ROUNDS[r]
                for par in range(2):
                    k = 2 * r + par
                    pool.wait_ge(w_hi, k + 1)
                    pool.tensor_tensor(weights(w, c, par, 1), split2(wf[:, r % 2, par, :], w),
                                       weights(w, c, par, 0).bitcast(F32), ALU.subtract).then_inc(w_lo, 1)

            inv_std(0)
            for r in range(len(ROUNDS)):
                w_low(r)
                if r == 7:
                    inv_std(1)
            with pool.Fori(0, TILES - 1) as i:
                inv_std(2 + i)
            pool.wait_ge(x_done, 2 * TILES)
            pool.memset(Vx[:, :, :, :, 3 * HD], 1.0).then_inc(vx_ones, 1)

            def v_rest(c, b):
                if not (isinstance(c, int) and c == 0):
                    pool.wait_ge(v_3, c)
                pool.wait_ge(v_1, c + 1)
                pool.tensor_tensor(v32[:], v32[:], Vx[:, b, :, :, 0:HD], ALU.subtract).then_inc(v_r, 1)
                pool.wait_ge(v_2, c + 1)
                pool.tensor_tensor(Vx[:, b, :, :, 2 * HD:3 * HD], v32[:], Vx[:, b, :, :, HD:2 * HD],
                                   ALU.subtract).then_inc(v_3, 1)

            def p_low(c, u):
                pool.wait_ge(ph_done, 8 * c + u + 1)
                if u >= RING:
                    pool.wait_ge(pv_done, 8 * c + u - RING + 1)
                pool.tensor_tensor(Pl[:, u % RING], Pf[:, u % RING], Ph[:, u % RING], ALU.subtract).then_inc(pl_pool, 1)

            def step(i, b, last):
                c = 2 * i + b
                more = not (last and b == 1)
                xt = X[:, bass.ts(c, 2), :]
                pool.tensor_tensor(xt, xt, bo_sb[:].unsqueeze(1).to_broadcast([P, 2, D]), ALU.add).then_inc(xb_done, 1)
                p_low(c, 2)
                p_low(c, 5)
                p_low(c, 6)
                if more:
                    p_low(c + 1, 0)
                if b == 1 and not last:
                    inv_std(TILES + 2 + i)
                if not last:
                    v_rest(c + 2, b)

            v_rest(0, 0)
            inv_std(TILES + 1)
            v_rest(1, 1)
            p_low(0, 0)
            with pool.Fori(0, TILES - 1) as i:
                for b in range(2):
                    step(i, b, False)
            for b in range(2):
                step(TILES - 1, b, True)
            with pool.Fori(0, TILES) as i:
                inv_std(2 * TILES + 1 + i)

        @block.scalar
        def _(act):
            def y_high(k, bank):
                for kt in range(KT):
                    act.wait_ge(xt_done, KT * k + kt + 1)
                    act.activation(yT[:, 0, kt, :], ps[:, bank[kt], :], ACT.Copy).then_inc(yh_done, 1)

            def w_high(r):
                w, c = ROUNDS[r]
                for par in range(2):
                    k = 2 * r + par
                    act.wait_ge(w_f, k + 1)
                    act.activation(weights(w, c, par, 0), split2(wf[:, r % 2, par, :], w), ACT.Copy).then_inc(w_hi, 1)

            def ffn_tile(t, k, first=False):
                for n in range(NT):
                    act.wait_ge(g_ready, NT * t + n + 1)
                    if n >= 2 or not first:
                        act.wait_ge(inter_done, NT * t + n - 1)
                    act.activation(gb[:, n % 2, :], ps[:, 4 + n % 2, :], ACT.Gelu_apprx_tanh).then_inc(gelu_done, 1)
                    if first and n == 0:
                        w_high(2)
                    if first and n - 1 in ROUND_AT:
                        w_high(ROUND_AT[n - 1])
                    act.wait_ge(inter_done, NT * t + n + 1)
                    if n == 0 and not first:
                        act.wait_ge(d_done, NT * t)
                    if n >= 3:
                        act.wait_ge(d_done, NT * t + n - 2)
                    act.activation(ih[:, n % 3, :], tb[:, n % 2, :], ACT.Copy).then_inc(hi_done, 1)
                y_high(k + 1, (4, 6))

            w_high(0)
            y_high(0, (4, 6))
            w_high(1)
            ffn_tile(0, 0, first=True)
            act.wait_ge(aux_in, 16)
            act.activation(auxr[:], auxs[:], ACT.Copy).then_inc(aux_r, 1)
            act.wait_ge(wa_in, 80)
            act.activation(WQ[:, 0, :, 0:D], wqs[:, :, 0:D], ACT.Copy, scale=0.25).then_inc(wa_hi, 1)
            act.activation(WQ[:, 0, :, D:3 * D], wqs[:, :, D:3 * D], ACT.Copy).then_inc(wa_hi, 1)
            act.activation(WO[:, 0, :, :], wos[:], ACT.Copy).then_inc(wa_hi, 1)
            with act.Fori(0, TILES - 1) as i:
                ffn_tile(1 + i, 1 + i)


            def qk_high(c, t, dst, bank):
                for b in range(2 * t, 2 * t + 2):
                    act.wait_ge(qk_ready, 4 * c + 2 * t + 2)
                    act.activation(dst[:, b, 0, :], ps[:, bank, S * (b % 2):S * (b % 2) + S], ACT.Identity,
                                   bias=bqk_s[:, b:b + 1]).then_inc(qk_hi, 1)

            def v_first(c, b):
                act.wait_ge(v_sum, c + 1)
                if not isinstance(c, int):
                    act.wait_ge(pv_done, 8 * (c - 1))
                act.activation(Vx[:, b, :, :, 0:HD], v32[:].rearrange("p t (h d) -> p t h d", h=H),
                               ACT.Copy).then_inc(v_1, 1)

            def v_second(c, b):
                act.wait_ge(v_r, c + 1)
                act.activation(Vx[:, b, :, :, HD:2 * HD], v32[:].rearrange("p t (h d) -> p t h d", h=H),
                               ACT.Copy).then_inc(v_2, 1)

            def max_copy(c, hf):
                act.wait_ge(mt_ready, 2 * c + hf + 1)
                act.activation(MT[:], ps[0:16, 7, 0:S], ACT.Copy).then_inc(mt_copied, 1)

            def exps(c, u):
                act.wait_ge(st_ready, 8 * c + u + 1)
                if u >= RING:
                    wait_p_low(act, c, u - RING)
                bank = st_bank(c, u)
                act.activation(Pf[:, u % RING], ps[:, bank:bank + 2, 0:384], ACT.Exp, bias=shift[:, 0:1]).then_inc(exp_done, 1)
                if u >= RING:
                    act.wait_ge(pv_done, 8 * c + u - RING + 1)
                act.wait_ge(exp_done, 8 * c + u + 1)
                act.activation(Ph[:, u % RING], Pf[:, u % RING], ACT.Copy).then_inc(ph_done, 1)

            def step(i, b, last):
                c = 2 * i + b
                more, qk = not (last and b == 1), not last
                if b == 0:
                    y_high(TILES + 1 + i, (6, 7))
                exps(c, 2)
                exps(c, 3)
                if qk:
                    act.wait_ge(stk[1 - b], 192 * (i + b + 1))
                    qk_high(c + 2, 0, HL, 6)
                exps(c, 4)
                exps(c, 5)
                exps(c, 6)
                if qk:
                    qk_high(c + 2, 1, HL, 7)
                exps(c, 7)
                if more:
                    act.wait_ge(m_rows[b][1], 32 * (i + 1))
                    max_copy(c + 1, 0)
                if more:
                    exps(c + 1, 0)
                if qk:
                    v_first(c + 2, b)
                act.wait_ge(ct_ready, c + 1)
                act.activation(CT[:, 0], ps[:, 7, :].rearrange("p (k t) -> p k t", k=KT), ACT.Copy).then_inc(ct_hi, 1)
                if more:
                    exps(c + 1, 1)
                if qk:
                    v_second(c + 2, b)
                if more:
                    act.wait_ge(m_rows[1 - b][0], 32 * (i + b + 1))
                    max_copy(c + 1, 1)

            for t in range(2):
                qk_high(0, t, HL, 6 + t)
            v_first(0, 0)
            qk_high(1, 0, HL1, 5)
            v_second(0, 0)
            qk_high(1, 1, HL1, 6)
            v_first(1, 1)
            v_second(1, 1)
            max_copy(0, 0)
            exps(0, 0)
            exps(0, 1)
            act.wait_ge(m_rows[0][0], 32)
            max_copy(0, 1)
            with act.Fori(0, TILES - 1) as i:
                for b in range(2):
                    step(i, b, False)
            for b in range(2):
                step(TILES - 1, b, True)
            with act.Fori(0, TILES) as i:
                ffn_tile(TILES + i, 2 * TILES + i)

        @block.vector
        def _(dve):
            def stats(k, tile):
                for s in range(SUB):
                    if isinstance(k, int) and k == 0 and s % 2 == 0:
                        dve.wait_ge(x_first[s // 2], 16)
                    dve.bn_stats(st6[:, s, :], X[:, bass.ds(SUB * tile + s, 1), :].rearrange("p s d -> p (s d)")).then_inc(bn1, 1)
                dve.wait_ge(bn1, SUB * (k + 1))
                dve.memset(carry[:], 0.0)
                for s in range(SUB):
                    dve.bn_aggr(mv[:, s, :], st6[:, s, :]).then_inc(bn2, 1)

            def normalise(k, tile):
                dve.wait_ge(rstd_done, k + 1)
                if not (isinstance(k, int) and k == 0):
                    dve.wait_ge(xt_done, KT * k)
                for s in range(SUB):
                    dve.tensor_scalar(yn[:, s, :], X[:, bass.ds(SUB * tile + s, 1), :].rearrange("p s d -> p (s d)"),
                                      mv[:, s, 0:1], rstd[:, s:s + 1], ALU.subtract, ALU.mult).then_inc(yn_done, 1)

            def y_low(k, bank):
                for kt in range(KT):
                    dve.wait_ge(yh_done, KT * k + kt + 1)
                    dve.tensor_tensor(yT[:, 1, kt, :], ps[:, bank[kt], :], yT[:, 0, kt, :].bitcast(F32),
                                      ALU.subtract).then_inc(yl_done, 1)

            def dequant(r):
                w, c = ROUNDS[r]
                u = r % 2
                dve.wait_ge(pk_in[u], 16 * (r // 2 + 1))
                for par in range(2):
                    dve.tensor_scalar(dT[:, par, :], pk[:, u, :], 28 - 4 * par, 19, ALU.logical_shift_left,
                                      ALU.arith_shift_right).then_inc(dec1, 1)
                for par in range(2):
                    dve.wait_ge(dec1, 2 * r + par + 1)
                    dve.tensor_scalar(dU[:, par, :], dT[:, par, :], 0x8E00, None, ALU.bitwise_and).then_inc(dec2, 1)
                dve.wait_ge(sc_in[u], 16 * (r // 2 + 1))
                for par in range(2):
                    dve.wait_ge(dec2, 2 * r + par + 1)
                    if r >= 2:
                        dve.wait_ge(w_lo, 2 * (r - 2) + par + 1)
                    dve.scalar_tensor_tensor(out=wf[:, r % 2, par, :], in0=dU[:, par, :].bitcast(F16)[:, 0::2],
                                             scalar=float(2 ** 14), in1=sc[:, u, :], op0=ALU.mult,
                                             op1=ALU.mult).then_inc(w_f, 1)

            def ffn_tile(t, k, tile, nxt, first=False):
                for n in range(NT):
                    dve.wait_ge(u_ready, NT * t + n + 1)
                    dve.wait_ge(gelu_done, NT * t + n + 1)
                    if n >= 2 or not first:
                        dve.wait_ge(hi_done, NT * t + n - 1)
                        dve.wait_ge(lo_done, NT * t + n - 1)
                    dve.tensor_tensor(tb[:, n % 2, :], ps[:, 6 + n % 2, :], gb[:, n % 2, :],
                                      ALU.mult).then_inc(inter_done, 1)
                    if first and n in ROUND_AT:
                        dequant(ROUND_AT[n])
                    dve.wait_ge(hi_done, NT * t + n + 1)
                    dve.tensor_tensor(il[:, n % 3, :], tb[:, n % 2, :], ih[:, n % 3, :].bitcast(F32),
                                      ALU.subtract).then_inc(lo_done, 1)
                    if first and n == 6:
                        dve.wait_ge(x_rest, 16)
                    if n == (7 if first else 4):
                        stats(k + 1, nxt)
                    if n == (11 if first else 7):
                        normalise(k + 1, nxt)
                y_low(k + 1, (4, 6))
                dve.wait_ge(d_done, NT * (t + 1))
                for part, done in ((0, xa_done), (1, x_done)):
                    for h in range(2):
                        xt = X[:, bass.ds(SUB * tile + 2 * h, 2), :]
                        if part == 1:
                            dve.wait_ge(xa_done, 2 * t + h + 1)
                        dve.scalar_tensor_tensor(out=xt, in0=ps[:, 2 * h:2 * h + 2, D * part:D * part + D], scalar=0.5,
                                                 in1=xt, op0=ALU.mult, op1=ALU.add).then_inc(done, 1)

            stats(0, 0)
            dequant(0)
            normalise(0, 0)
            dequant(1)
            y_low(0, (4, 6))
            dequant(2)
            ffn_tile(0, 0, 0, 1, first=True)
            dve.wait_ge(wa_in, 80)
            dve.wait_ge(wa_hi, 3)
            dve.scalar_tensor_tensor(out=WQ[:, 1, :, 0:D], in0=wqs[:, :, 0:D], scalar=0.25,
                                     in1=WQ[:, 0, :, 0:D].bitcast(F32), op0=ALU.mult, op1=ALU.subtract).then_inc(wa_lo, 1)
            dve.tensor_tensor(WQ[:, 1, :, D:3 * D], wqs[:, :, D:3 * D], WQ[:, 0, :, D:3 * D].bitcast(F32),
                              ALU.subtract).then_inc(wa_lo, 1)
            dve.tensor_tensor(WO[:, 1], wos[:], WO[:, 0].bitcast(F32), ALU.subtract).then_inc(wa_lo, 1)
            dve.tensor_scalar(bqk_s[:, 0:2], bqk_sb[:, 0:2], 0.25, None, ALU.mult).then_inc(wa_lo, 1)
            dve.tensor_copy(bqk_s[:, 2:4], bqk_sb[:, 2:4]).then_inc(wa_lo, 1)
            with dve.Fori(0, TILES - 1) as i:
                ffn_tile(1 + i, 1 + i, 1 + i, (i + 2) & (TILES - 1))

            def qk_low(c, t, dst, bank):
                for b in range(2 * t, 2 * t + 2):
                    dve.wait_ge(qk_hi, 4 * c + 2 * t + 2)
                    dve.scalar_tensor_tensor(out=dst[:, b, 1, :], in0=ps[:, bank, S * (b % 2):S * (b % 2) + S],
                                             scalar=bqk_s[:, b:b + 1], in1=dst[:, b, 0, :].bitcast(F32),
                                             op0=ALU.add, op1=ALU.subtract).then_inc(qk_lo, 1)

            def v_add(c, bank=6):
                if not (isinstance(c, int) and c == 0):
                    dve.wait_ge(v_3, c)
                dve.wait_ge(v_ready, c + 1)
                dve.tensor_tensor(v32[:], ps[:, bank, :].rearrange("p (t d) -> p t d", t=2),
                                  bv_sb[:].unsqueeze(1).to_broadcast([P, 2, D]), ALU.add).then_inc(v_sum, 1)

            def maxima(c, p, bank=0):
                hf, pp = p // HALF, p % HALF
                dve.wait_ge(s_ready, 8 * c + p + 1)
                dve.tensor_reduce(mx[:, hf, 1, :, pp], ps[:, bank:bank + 2, 0:256], AX.X, ALU.max)
                dve.tensor_reduce(mx[:, hf, 0, :, pp], ps[:, bank:bank + 2, 256:384], AX.X, ALU.max).then_inc(mx_done, 1)

            def neg_max_high(c, hf):
                dve.wait_ge(mx_done, 8 * c + 4 * hf + 4)
                dve.tensor_scalar(NM[:, hf, :, :, 0, :].bitcast(F32R), mx[:, hf], -1.0, None, ALU.mult).then_inc(nm_done, 1)

            def neg_max_low(c, hf):
                dve.wait_ge(nm_done, 4 * c + 2 * hf + 1)
                dve.scalar_tensor_tensor(out=NM[:, hf, :, :, 1, :].bitcast(F32R), in0=mx[:, hf], scalar=-1.0,
                                         in1=NM[:, hf, :, :, 0, :], op0=ALU.mult, op1=ALU.subtract).then_inc(nm_done, 1)

            def p_low(c, u):
                if u in POOL_PAIRS:
                    return
                dve.wait_ge(ph_done, 8 * c + u + 1)
                if u >= RING:
                    dve.wait_ge(pv_done, 8 * c + u - RING + 1)
                dve.tensor_tensor(Pl[:, u % RING], Pf[:, u % RING], Ph[:, u % RING], ALU.subtract).then_inc(pl_dve, 1)

            def context(c, hf):
                k = 2 * c + hf
                dve.wait_ge(pv_done, 4 * k + 4)
                for qt in range(2):
                    o = ps[:, 4 + qt, 0:8 * VP].rearrange("p (h v) -> p h v", v=VP)
                    dve.tensor_reduce(cs[:, qt], o[:, :, 0:3 * HD].rearrange("p h (t d) -> p h d t", t=3),
                                      AX.X, ALU.add).then_inc(red_done, 1)
                o = ps[:, 4:6, 0:8 * VP].rearrange("p q (h v) -> p q h v", v=VP)
                dve.reciprocal(rc[:], o[:, :, :, 3 * HD]).then_inc(rc_done, 1)

            def context_scaled(c, hf):
                k = 2 * c + hf
                dve.wait_ge(red_done, 2 * k + 2)
                dve.wait_ge(rc_done, k + 1)
                dve.tensor_tensor(cx[:, :, P * hf:P * hf + P].rearrange("p q (h d) -> p q h d", h=8), cs[:],
                                  rc[:].unsqueeze(3).to_broadcast([P, 2, 8, HD]), ALU.mult).then_inc(cx_done, 1)

            def step(i, b, last):
                c = 2 * i + b
                more, qk = not (last and b == 1), not last
                def a_unit(v):
                    if more:
                        maxima(c + 1, v)

                if b == 0:
                    y_low(TILES + 1 + i, (6, 7))
                p_low(c, 1)
                p_low(c, 2)
                a_unit(0)
                p_low(c, 3)
                if qk:
                    qk_low(c + 2, 0, HL, 6)
                a_unit(1)
                p_low(c, 4)
                a_unit(2)
                context(c, 0)
                p_low(c, 5)
                a_unit(3)
                if more:
                    neg_max_high(c + 1, 0)
                context_scaled(c, 0)
                if qk:
                    qk_low(c + 2, 1, HL, 7)
                if more:
                    neg_max_low(c + 1, 0)
                a_unit(4)
                if b == 1 and not last:
                    stats(TILES + 2 + i, (i + 2) & (TILES - 1))
                p_low(c, 6)
                p_low(c, 7)
                a_unit(5)
                if qk:
                    v_add(c + 2)
                context(c, 1)
                context_scaled(c, 1)
                a_unit(6)
                dve.wait_ge(ct_hi, c + 1)
                dve.tensor_tensor(CT[:, 1], ps[:, 7, :].rearrange("p (k t) -> p k t", k=KT),
                                  CT[:, 0].bitcast(F32), ALU.subtract).then_inc(ct_lo, 1)
                if more:
                    p_low(c + 1, 0)
                a_unit(7)
                if more:
                    neg_max_high(c + 1, 1)
                if b == 1 and not last:
                    normalise(TILES + 2 + i, (i + 2) & (TILES - 1))
                if more:
                    neg_max_low(c + 1, 1)
                xt = X[:, bass.ts(c, 2), :]
                dve.wait_ge(xb_done, c + 1)
                dve.wait_ge(o_ready, c + 1)
                dve.tensor_tensor(xt, xt, ps[:, out_bank(c), :].rearrange("p (t d) -> p t d", t=2), ALU.add).then_inc(ax_done, 1)

            dve.sem_inc(ax_done, 1)
            for t in range(2):
                qk_low(0, t, HL, 6 + t)
            v_add(0, 4)
            qk_low(1, 0, HL1, 5)
            qk_low(1, 1, HL1, 6)
            stats(TILES + 1, 1)
            v_add(1, 7)
            normalise(TILES + 1, 1)
            for p in range(PAIRS):
                maxima(0, p, 4 * (p % 2))
                if p % HALF == HALF - 1:
                    neg_max_high(0, p // HALF)
                    neg_max_low(0, p // HALF)
            p_low(0, 0)
            with dve.Fori(0, TILES - 1) as i:
                for b in range(2):
                    step(i, b, False)
            for b in range(2):
                step(TILES - 1, b, True)
            with dve.Fori(0, TILES) as i:
                ffn_tile(TILES + i, 2 * TILES + i, i, (i + 1) & (TILES - 1))

        @block.tensor
        def _(pe):
            def transpose_y(k, bank):
                pe.wait_ge(yn_done, SUB * (k + 1))
                for kt in range(KT):
                    for s in range(SUB):
                        mm = pe.transpose(ps[:, bank[kt], P * s:P * s + P], yn[:, s, kt::KT], ident[:, :])
                    mm.then_inc(xt_done, 1)

            def product(out, w, col, rhs_h, rhs_l, start=True):
                for kt in range(KT):
                    for j, (a, b) in enumerate(((0, rhs_h), (1, rhs_h), (0, rhs_l))):
                        mm = pe.matmul(out, w[:, a, kt, col], b(kt), start=(kt == 0 and j == 0),
                                       stop=(kt == KT - 1 and j == 2))
                return mm

            def down(t, n, first):
                pe.wait_ge(hi_done, NT * t + n + 1)
                pe.wait_ge(lo_done, NT * t + n + 1)
                if n == 0 and not first:
                    pe.wait_ge(x_done, 2 * t)
                for s in range(SUB):
                    tok = slice(P * s, P * s + P)
                    pe.matmul(ps[:, s, :], ih[:, n % 3, tok], WD[:, n, :, :], start=(n == 0), stop=False,
                              skip_group_check=True)
                    mm = pe.matmul(ps[:, s, 0:D], il[:, n % 3, tok], WD[:, n, 0, :], start=False,
                                   stop=(n == NT - 1), skip_group_check=True)
                mm.then_inc(d_done, 1)

            def ffn_tile(t, k, first=False):
                pe.wait_ge(yh_done, KT * (k + 1))
                pe.wait_ge(yl_done, KT * (k + 1))
                yh, yl = (lambda kt: yT[:, 0, kt, :]), (lambda kt: yT[:, 1, kt, :])
                for n in range(NT):
                    col = slice(P * n, P * n + P)
                    if first and n % NCH == 0:
                        pe.wait_ge(w_lo, 6 * (n // NCH) + 2)
                    if n >= 2 or not first:
                        pe.wait_ge(gelu_done, NT * t + n - 1)
                    product(ps[:, 4 + n % 2, :], WG, col, yh, yl).then_inc(g_ready, 1)
                    if first and n % NCH == 0:
                        pe.wait_ge(w_lo, 6 * (n // NCH) + 4)
                    if n >= 2 or not first:
                        pe.wait_ge(inter_done, NT * t + n - 1)
                    product(ps[:, 6 + n % 2, :], WU, col, yh, yl).then_inc(u_ready, 1)
                    if n == NT - 1:
                        pe.wait_ge(gelu_done, NT * t + NT - 1)
                        pe.wait_ge(inter_done, NT * t + NT - 1)
                        transpose_y(k + 1, (4, 6))
                    if n >= 2:
                        if first and (n - 2) % NCH == 0:
                            pe.wait_ge(w_lo, 6 * ((n - 2) // NCH) + 6)
                        down(t, n - 2, first)
                down(t, NT - 2, first)
                down(t, NT - 1, first)

            pe.wait_ge(const_done, 4)
            transpose_y(0, (4, 6))
            ffn_tile(0, 0, first=True)
            with pe.Fori(0, TILES - 1) as i:
                ffn_tile(1 + i, 1 + i)

            pe.wait_ge(wa_lo, 5)
            pe.wait_ge(gelu_done, NT * TILES)
            pe.wait_ge(inter_done, NT * TILES)

            def qk_project(c, b, t, bank, heads=range(2)):
                tok = slice(S * b, S * b + S)
                for a in heads:
                    r = P * (2 * t + a)
                    product(ps[:, bank, S * a:S * a + S], WQ, slice(r, r + P),
                            lambda kt: yT[:, 0, kt, tok], lambda kt: yT[:, 1, kt, tok]).then_inc(qk_ready, 1)

            def v_project(c, b, bank=6):
                for t in range(2):
                    tok = slice(S * b + P * t, S * b + P * t + P)
                    for kt in range(KT):
                        for j, (a, w) in enumerate(((0, 0), (0, 1), (1, 0))):
                            mm = pe.matmul(ps[:, bank, D * t:D * t + D], yT[:, a, kt, tok], WQ[:, w, kt, 2 * D:3 * D],
                                           start=(kt == 0 and j == 0), stop=(kt == KT - 1 and j == 2))
                mm.then_inc(v_ready, 1)

            def scores(c, b, p, n, bank=0):
                if p == 0:
                    pe.wait_ge(stk[b], 192 * n)
                if not (isinstance(c, int) and c == 0):
                    pe.wait_ge(mx_done, 8 * c + p)
                elif p >= 2:
                    pe.wait_ge(mx_done, p - 1)
                for a in range(2):
                    r = slice(64 * a, 64 * a + 50)
                    pe.matmul(ps[:, bank + a, 0:256], QS[r, b, p, P:2 * P], KS[r, b, p, 0:2 * P], start=True, stop=False,
                              skip_group_check=True)
                    pe.matmul(ps[:, bank + a, 256:384], QS[r, b, p, 0:P], KS[r, b, p, 0:P], start=False, stop=False,
                              skip_group_check=True)
                for a in range(2):
                    mm = pe.matmul(ps[:, bank + a, 128:384], identb[:, :], mask[:].rearrange("p a b -> p (a b)"),
                                   start=False, stop=True, skip_group_check=True)
                mm.then_inc(s_ready, 1)

            def transpose_max(c, hf):
                k = 2 * c + hf
                pe.wait_ge(nm_done, 2 * k + 2)
                for qt in range(2):
                    mm = pe.transpose(ps[0:16, 7, P * qt:P * qt + P],
                                      NM[:, hf, qt].rearrange("p a l h -> p (a l h)"), ident[:, :])
                mm.then_inc(mt_ready, 1)

            def scores_t(c, b, p, n):
                if p % HALF == 0:
                    pe.wait_ge(m_rows[b][p // HALF], 32 * n)
                bank = st_bank(c, p)
                if isinstance(c, int) and c == B - 1 and p >= 2:
                    pe.wait_ge(exp_done, 8 * c + p - 1)
                    pe.wait_ge(mx_done, 8 * B)
                elif p >= 1:
                    pe.wait_ge(exp_done, 8 * c + p)
                for a in range(2):
                    r = slice(64 * a, 64 * a + 52)
                    pe.matmul(ps[:, bank + a, 128:384], KS[r, b, p, 0:P], QS[r, b, p, 0:2 * P], start=True, stop=False,
                              skip_group_check=True)
                    pe.matmul(ps[:, bank + a, 0:128], KS[r, b, p, P:2 * P], QS[r, b, p, P:2 * P], start=False, stop=False,
                              skip_group_check=True)
                for a in range(2):
                    mm = pe.matmul(ps[:, bank + a, 0:256], identb[:, :], maskT[:].rearrange("p a b -> p (a b)"),
                                   start=False, stop=True, skip_group_check=True)
                mm.then_inc(st_ready, 1)

            def values(c, b, p):
                if p == 0:
                    pe.wait_ge(v_3, c + 1)
                if p == HALF:
                    pe.wait_ge(rc_done, 2 * c + 1)
                    pe.wait_ge(red_done, 4 * c + 2)
                wait_p_low(pe, c, p)
                for a in range(2):
                    h = 2 * p + a
                    o = slice(VP * (h % 8), VP * (h % 8) + VP)
                    for qt, kt, col in ((0, 0, 128), (1, 0, 256), (1, 1, 0)):
                        for j, src in enumerate((Ph, Pl)):
                            mm = pe.matmul(ps[:, 4 + qt, o], src[:, p % RING, a, col:col + P], Vx[:, b, kt, h, 0:VP],
                                           start=(h % 8 == 0 and kt == 0 and j == 0), stop=(kt == qt and j == 1),
                                           skip_group_check=True)
                mm.then_inc(pv_done, 1)

            def transpose_ctx(c):
                pe.wait_ge(cx_done, 2 * c + 2)
                for kt in range(KT):
                    for t in range(2):
                        mm = pe.transpose(ps[:, 7, S * kt + P * t:S * kt + P * t + P], cx[:, t, P * kt:P * kt + P],
                                          ident[:, :])
                mm.then_inc(ct_ready, 1)

            def out_project(c, bank):
                pe.wait_ge(ct_lo, c + 1)
                for t in range(2):
                    for kt in range(KT):
                        for j, (a, w) in enumerate(((0, 0), (0, 1), (1, 0))):
                            mm = pe.matmul(ps[:, bank, D * t:D * t + D], CT[:, a, kt, P * t:P * t + P], WO[:, w, kt, :],
                                           start=(kt == 0 and j == 0), stop=(kt == KT - 1 and j == 2))
                mm.then_inc(o_ready, 1)

            def step(i, b, last):
                c = 2 * i + b
                more, qk = not (last and b == 1), not last

                def a_unit(v):
                    if more:
                        scores(c + 1, 1 - b, v, i + b + 1)

                def qk_piece(t, a):
                    if qk:
                        qk_project(c + 2, b, t, 6 + t, (a,))

                scores_t(c, b, 2, i + 1)
                if b == 0:
                    pe.wait_ge(mt_copied, 2 * c + 2)
                    pe.wait_ge(ax_done, c + 1)
                    transpose_y(TILES + 1 + i, (6, 7))
                values(c, b, 0)
                a_unit(0)
                scores_t(c, b, 3, i + 1)
                if qk:
                    if b == 0:
                        pe.wait_ge(yh_done, KT * (TILES + 2 + i))
                        pe.wait_ge(yl_done, KT * (TILES + 2 + i))
                    else:
                        pe.wait_ge(ax_done, c + 1)
                    qk_piece(0, 0)
                qk_piece(0, 1)
                scores_t(c, b, 4, i + 1)
                a_unit(1)
                values(c, b, 1)
                values(c, b, 2)
                scores_t(c, b, 5, i + 1)
                if qk:
                    if b == 1:
                        pe.wait_ge(mt_copied, 2 * c + 2)
                    qk_piece(1, 0)
                a_unit(2)
                scores_t(c, b, 6, i + 1)
                values(c, b, 3)
                a_unit(3)
                qk_piece(1, 1)
                scores_t(c, b, 7, i + 1)
                values(c, b, 4)
                a_unit(4)
                if qk:
                    pe.wait_ge(qk_lo, 4 * c + 12)
                elif b == 0:
                    pe.wait_ge(yl_done, KT * (TILES + 2 + i))
                if more:
                    transpose_max(c + 1, 0)
                if qk:
                    pe.wait_ge(qk_lo, 4 * c + 10)
                    v_project(c + 2, b)
                values(c, b, 5)
                a_unit(5)
                values(c, b, 6)
                values(c, b, 7)
                if more:
                    scores_t(c + 1, 1 - b, 0, i + b + 1)
                a_unit(6)
                if more:
                    scores_t(c + 1, 1 - b, 1, i + b + 1)
                if more:
                    pe.wait_ge(mt_copied, 2 * c + 3)
                else:
                    pe.wait_ge(mt_copied, 2 * c + 2)
                transpose_ctx(c)
                a_unit(7)
                if qk:
                    pe.wait_ge(v_sum, c + 3)
                elif b == 0:
                    pe.wait_ge(yl_done, KT * (TILES + 2 + i))
                out_project(c, out_bank(c))
                if more:
                    transpose_max(c + 1, 1)

            pe.wait_ge(yh_done, KT * (TILES + 1))
            pe.wait_ge(yl_done, KT * (TILES + 1))
            qk_project(0, 0, 0, 6)
            qk_project(0, 0, 1, 7)
            v_project(0, 0, 4)
            qk_project(1, 1, 0, 5)
            pe.wait_ge(qk_lo, 2)
            qk_project(1, 1, 1, 6)
            pe.wait_ge(qk_lo, 4)
            v_project(1, 1, 7)
            pe.wait_ge(x_done, 2 * TILES)
            pe.wait_ge(aux_st, 128)
            for p in range(PAIRS):
                if p == 1:
                    pe.wait_ge(v_sum, 1)
                    pe.wait_ge(qk_lo, 6)
                scores(0, 0, p, 1, 4 * (p % 2))
                if p == HALF:
                    pe.wait_ge(qk_lo, 8)
                    pe.wait_ge(v_sum, 2)
                    transpose_max(0, 0)
                if p == PAIRS - 2:
                    scores_t(0, 0, 0, 1)
            scores_t(0, 0, 1, 1)
            pe.wait_ge(mt_copied, 1)
            transpose_max(0, 1)
            pe.wait_ge(vx_ones, 1)
            with pe.Fori(0, TILES - 1) as i:
                for b in range(2):
                    step(i, b, False)
            for b in range(2):
                step(TILES - 1, b, True)

            with pe.Fori(0, TILES) as i:
                ffn_tile(TILES + i, 2 * TILES + i)


def _bits12(v):
    b = v.astype(np.float32).view(np.uint32)
    return ((b + 0x7FF + ((b >> 12) & 1)) & np.uint32(0xFFFFF000)).view(np.float32)


def _stack_constants():
    pos = np.arange(1 - S, 1, dtype=np.float32)
    m = np.arange(1, H + 1, dtype=np.float32) * np.float32(8.0 / H)
    slopes = (np.float32(1.0) / np.float32(2.0) ** m).astype(np.float32)
    bias = (pos[None, :] * slopes[:, None]).astype(np.float32)
    hi = _bits12(bias)
    lo = bias - hi
    rows = np.ones((16, PAIRS, S), np.float32)
    for a in range(2):
        rows[4 * a] = hi[a::2]
        rows[4 * a + 1] = lo[a::2]
    return rows


def kernel(**inputs):
    import concourse.bacc as bacc
    from concourse.bass_utils import run_bass_kernel_spmd

    a = {k: np.asarray(v) for k, v in inputs.items()}
    cont = np.ascontiguousarray
    blk = MLP // (2 * P)

    def columns(w):
        return cont(w.T.reshape(w.shape[1], blk, P, 2).transpose(0, 1, 3, 2).reshape(w.shape[1], MLP))

    def spread(s):
        return cont(np.repeat(s, P // s.shape[0], axis=0))

    dpk = a["L0_ffn_down_W_packed"]
    dsc = a["L0_ffn_down_scales"]
    W = a["L0_attn_Wqkv"]
    bq = a["L0_attn_b_qkv"]

    def by_parity(m):
        return m.reshape(PAIRS, 2, HD, -1).transpose(1, 2, 0, 3).reshape(D, -1)

    Wr = np.concatenate([by_parity(W[0:D]), by_parity(W[D:2 * D]), W[2 * D:]])
    bqk = np.concatenate([by_parity(bq[0:D]), by_parity(bq[D:2 * D])]).reshape(4, P).T
    arrays = {
        "in_x": cont(a["L0_attn_x"]),
        "in_gate_pk": columns(a["L0_ffn_gate_W_packed"]),
        "in_gate_sc": spread(columns(a["L0_ffn_gate_scales"])),
        "in_up_pk": columns(a["L0_ffn_up_W_packed"]),
        "in_up_sc": spread(columns(a["L0_ffn_up_scales"])),
        "in_down_pk": cont(dpk.T.reshape(blk, P, D).transpose(1, 0, 2).reshape(P, MLP)),
        "in_down_sc": spread(cont(dsc.T.reshape(blk, 8, D).transpose(1, 0, 2).reshape(8, MLP))),
        "in_wqkv": cont(Wr.T.reshape(P, KT, 3 * D)),
        "in_bqk": cont(bqk),
        "in_bv": cont(bq[2 * D:]),
        "in_wout": cont(a["L0_attn_Wout"].T.reshape(KT, P, D).transpose(1, 0, 2)),
        "in_bout": cont(a["L0_attn_b_out"]),
        "in_aux": _stack_constants(),
    }
    nc = bacc.Bacc("TRN2", target_bir_lowering=False, num_devices=1, dynamic_dma_scratch_size=4096)
    args = [nc.dram_tensor(n, v.shape, mybir.dt.from_np(v.dtype), kind="ExternalInput").ap()
            for n, v in arrays.items()]
    args.append(nc.dram_tensor("out_0", (B, S, D), F32, kind="ExternalOutput").ap())
    macaron_kernel(nc, *args)
    r = run_bass_kernel_spmd(nc, [arrays], core_ids=[0])
    return r.results[0]["out_0"]
```
